# Optimizing a Trainium2 kernel written in Bass

```python
import numpy as np
import jax
import jax.numpy as jnp

def _softmax(x, axis=-1):
    return jax.nn.softmax(x, axis=axis)

def _gelu(x):
    return jax.nn.gelu(x, approximate=True)

def _silu(x):
    return jax.nn.silu(x)

def _sigmoid(x):
    return jax.nn.sigmoid(x)

def _layernorm(x, axis=-1, eps=1e-05):
    m = jnp.mean(x, axis=axis, keepdims=True)
    v = jnp.var(x, axis=axis, keepdims=True)
    return (x - m) / jnp.sqrt(v + eps)

def _scatter_add(tgt, idx, src, axis=0):
    return tgt.at[idx].add(src)

def _segment_sum(src, seg, n):
    return jax.ops.segment_sum(src, seg, n)
kernel_name = 'mk_seq_preln_d1_jaxref_r4_4589a2'

def setup_inputs(seed: int=0):
    np.random.seed(seed)
    _w = jnp.asarray

    def _L0_attn_setup():
        import jax, jax.numpy as jnp
        import numpy as np
        B, T, D = (1, 512, 512)
        H, DK, DV, M = (16, 64, 128, 64)
        KEY_DIM, VALUE_DIM = (H * DK, H * DV)
        EPS = 1e-05
        CLAMP_MIN, CLAMP_MAX = (-32.0, 32.0)
        XAVIER_GAIN = 2.0 ** (-2.5)

        def _chunk_abc(q, k, v, s):
            scale = q.shape[-1] ** (-0.5)
            z = jax.lax.cumlogsumexp(s, axis=2)
            g = jnp.exp(jnp.concatenate([z[:, :, :1], z[:, :, :-1]], axis=2) - z)
            p = jnp.exp(s - z)
            tfirst = lambda x: jnp.moveaxis(x, 2, 0)
            qT, kT, vT, pT, gT = map(tfirst, (q * scale, k, v, p, g))
            b, h = (q.shape[0], q.shape[1])
            hk0 = jnp.zeros((b, h, q.shape[-1], s.shape[-1]), q.dtype)

            def step_k(hk, x):
                q_t, k_t, p_t, g_t = x
                hk = hk * g_t[:, :, None, :] + k_t[..., None] * p_t[:, :, None, :]
                return (hk, jnp.einsum('bhk,bhkm->bhm', q_t, hk))
            _, okT = jax.lax.scan(step_k, hk0, (qT, kT, pT, gT))
            pvT = jax.nn.softmax(okT, axis=-1)
            hv0 = jnp.zeros((b, h, s.shape[-1], v.shape[-1]), q.dtype)

            def step_v(hv, x):
                pv_t, v_t, p_t, g_t = x
                hv = hv * g_t[..., None] + p_t[..., None] * v_t[:, :, None, :]
                return (hv, jnp.einsum('bhm,bhmv->bhv', pv_t, hv))
            _, ovT = jax.lax.scan(step_v, hv0, (pvT, vT, pT, gT))
            return jnp.moveaxis(ovT, 0, 2)
        key = jax.random.key(seed)
        ks = jax.random.split(key, 8)

        def w(k, fan_in, fan_out):
            std = XAVIER_GAIN * np.sqrt(2.0 / (fan_in + fan_out))
            return jax.random.normal(k, (fan_in, fan_out), jnp.float32) * std
        return {'hidden_states': jax.random.normal(ks[0], (B, T, D), jnp.float32), 'Wq': w(ks[1], D, KEY_DIM), 'Wk': w(ks[2], D, KEY_DIM), 'Wv': w(ks[3], D, VALUE_DIM), 'Wg': w(ks[4], D, VALUE_DIM), 'Ws': w(ks[5], D, H * M), 'Wo': w(ks[6], VALUE_DIM, D), 'g_norm_weight': jnp.ones((DV,), jnp.float32)}
    _L0_attn_in = _L0_attn_setup()

    def _L0_ffn_setup():
        import jax, jax.numpy as jnp
        import numpy as np
        B, S, H, I = (1, 64, 512, 1536)

        def _quantized_matmul(x, w, scale):
            wq = w.astype(jnp.float8_e4m3fn).astype(x.dtype)
            y = jnp.einsum('bsi,io->bso', x, wq)
            return y * scale
        key = jax.random.key(seed)
        ks = jax.random.split(key, 7)
        return {'x': jax.random.normal(ks[0], (B, S, H), dtype=jnp.float32), 'gate_w': jax.random.normal(ks[1], (H, I), dtype=jnp.float32) * 0.02, 'up_w': jax.random.normal(ks[2], (H, I), dtype=jnp.float32) * 0.02, 'down_w': jax.random.normal(ks[3], (I, H), dtype=jnp.float32) * 0.02, 'gate_scale': jax.random.uniform(ks[4], (I,), dtype=jnp.float32, minval=0.5, maxval=1.5), 'up_scale': jax.random.uniform(ks[5], (I,), dtype=jnp.float32, minval=0.5, maxval=1.5), 'down_scale': jax.random.uniform(ks[6], (H,), dtype=jnp.float32, minval=0.5, maxval=1.5)}
    _L0_ffn_in = _L0_ffn_setup()
    _d = {'L0_attn_hidden_states': _L0_attn_in['hidden_states'], 'L0_attn_Wq': _L0_attn_in['Wq'], 'L0_attn_Wk': _L0_attn_in['Wk'], 'L0_attn_Wv': _L0_attn_in['Wv'], 'L0_attn_Wg': _L0_attn_in['Wg'], 'L0_attn_Ws': _L0_attn_in['Ws'], 'L0_attn_Wo': _L0_attn_in['Wo'], 'L0_attn_g_norm_weight': _L0_attn_in['g_norm_weight'], 'L0_ffn_gate_w': _L0_ffn_in['gate_w'], 'L0_ffn_up_w': _L0_ffn_in['up_w'], 'L0_ffn_down_w': _L0_ffn_in['down_w'], 'L0_ffn_gate_scale': _L0_ffn_in['gate_scale'], 'L0_ffn_up_scale': _L0_ffn_in['up_scale'], 'L0_ffn_down_scale': _L0_ffn_in['down_scale']}
    _x0 = _d['L0_attn_hidden_states']
    _d['L0_attn_hidden_states'] = jax.random.normal(jax.random.fold_in(jax.random.key(seed), 1), (4, 512, 512), dtype=_x0.dtype)
    del _x0
    return _d

def reference(L0_attn_hidden_states, L0_attn_Wq, L0_attn_Wk, L0_attn_Wv, L0_attn_Wg, L0_attn_Ws, L0_attn_Wo, L0_attn_g_norm_weight, L0_ffn_gate_w, L0_ffn_up_w, L0_ffn_down_w, L0_ffn_gate_scale, L0_ffn_up_scale, L0_ffn_down_scale):

    def _L0_attn_ref(hidden_states, Wq, Wk, Wv, Wg, Ws, Wo, g_norm_weight):
        import jax, jax.numpy as jnp
        import numpy as np
        B, T, D = (1, 512, 512)
        H, DK, DV, M = (16, 64, 128, 64)
        KEY_DIM, VALUE_DIM = (H * DK, H * DV)
        EPS = 1e-05
        CLAMP_MIN, CLAMP_MAX = (-32.0, 32.0)
        XAVIER_GAIN = 2.0 ** (-2.5)

        def _chunk_abc(q, k, v, s):
            scale = q.shape[-1] ** (-0.5)
            z = jax.lax.cumlogsumexp(s, axis=2)
            g = jnp.exp(jnp.concatenate([z[:, :, :1], z[:, :, :-1]], axis=2) - z)
            p = jnp.exp(s - z)
            tfirst = lambda x: jnp.moveaxis(x, 2, 0)
            qT, kT, vT, pT, gT = map(tfirst, (q * scale, k, v, p, g))
            b, h = (q.shape[0], q.shape[1])
            hk0 = jnp.zeros((b, h, q.shape[-1], s.shape[-1]), q.dtype)

            def step_k(hk, x):
                q_t, k_t, p_t, g_t = x
                hk = hk * g_t[:, :, None, :] + k_t[..., None] * p_t[:, :, None, :]
                return (hk, jnp.einsum('bhk,bhkm->bhm', q_t, hk))
            _, okT = jax.lax.scan(step_k, hk0, (qT, kT, pT, gT))
            pvT = jax.nn.softmax(okT, axis=-1)
            hv0 = jnp.zeros((b, h, s.shape[-1], v.shape[-1]), q.dtype)

            def step_v(hv, x):
                pv_t, v_t, p_t, g_t = x
                hv = hv * g_t[..., None] + p_t[..., None] * v_t[:, :, None, :]
                return (hv, jnp.einsum('bhm,bhmv->bhv', pv_t, hv))
            _, ovT = jax.lax.scan(step_v, hv0, (pvT, vT, pT, gT))
            return jnp.moveaxis(ovT, 0, 2)
        b, t, _ = hidden_states.shape
        to_heads = lambda x, d: jnp.transpose(x.reshape(b, t, H, d), (0, 2, 1, 3))
        q = to_heads(hidden_states @ Wq, DK)
        k = to_heads(hidden_states @ Wk, DK)
        v = to_heads(hidden_states @ Wv, DV)
        s = jnp.clip(to_heads(hidden_states @ Ws, M), CLAMP_MIN, CLAMP_MAX)
        o = jnp.transpose(_chunk_abc(q, k, v, s), (0, 2, 1, 3))
        g = (hidden_states @ Wg).reshape(b, t, H, DV)
        o = o * jax.lax.rsqrt(jnp.mean(jnp.square(o), axis=-1, keepdims=True) + EPS) * g_norm_weight
        o = o * (g * jax.nn.sigmoid(g))
        return o.reshape(b, t, VALUE_DIM) @ Wo

    def _L0_ffn_ref(x, gate_w, up_w, down_w, gate_scale, up_scale, down_scale):
        import jax, jax.numpy as jnp
        import numpy as np
        B, S, H, I = (1, 64, 512, 1536)

        def _quantized_matmul(x, w, scale):
            wq = w.astype(jnp.float8_e4m3fn).astype(x.dtype)
            y = jnp.einsum('bsi,io->bso', x, wq)
            return y * scale
        gate = jax.nn.silu(_quantized_matmul(x, gate_w, gate_scale))
        up = _quantized_matmul(x, up_w, up_scale)
        fuse = gate * up
        return _quantized_matmul(fuse, down_w, down_scale)
    x = L0_attn_hidden_states
    x = x + _L0_attn_ref(_layernorm(x, axis=-1), L0_attn_Wq, L0_attn_Wk, L0_attn_Wv, L0_attn_Wg, L0_attn_Ws, L0_attn_Wo, L0_attn_g_norm_weight)
    x = x + _L0_ffn_ref(_layernorm(x, axis=-1), L0_ffn_gate_w, L0_ffn_up_w, L0_ffn_down_w, L0_ffn_gate_scale, L0_ffn_up_scale, L0_ffn_down_scale)
    return x

_drawn_inputs = setup_inputs


def setup_inputs(seed=0):
    import zlib

    import numpy as np

    out = dict(_drawn_inputs(seed))
    spreads = {'L0_attn_g_norm_weight': (1.0, 0.6)}
    factors = {'L0_attn_Wq': 8.0,
     'L0_attn_Wk': 8.0,
     'L0_attn_Wv': 4.799,
     'L0_attn_Wg': 4.776,
     'L0_attn_Ws': 8.0,
     'L0_attn_Wo': 4.773}
    for name, (base, spread) in spreads.items():
        noise = np.random.default_rng([zlib.crc32(name.encode()), seed]).standard_normal(out[name].shape)
        drawn = base * np.exp(spread * noise) if base else spread * noise
        out[name] = jnp.asarray(drawn.astype(out[name].dtype))
    for name, factor in factors.items():
        out[name] = (out[name] * factor).astype(out[name].dtype)
    return out
```

```python
from contextlib import ExitStack

import concourse.bass as bass
from concourse import mybir
from concourse.alu_op_type import AluOpType as ALU

F32 = mybir.dt.float32
F32R = mybir.dt.float32r
I32 = mybir.dt.int32
ACT = mybir.ActivationFunctionType
AX = mybir.AxisListType

P = 128
B, T, D = 4, 512, 512
H, DK, DV, M = 16, 64, 128, 64
F = 1536
KT = D // P
CH = T // P
PAIRS = H // 2
UNITS = PAIRS * B
TILES = B * CH
FT = F // P
EPS = 1e-5
CLAMP = 32.0
SCALE = DK ** -0.5
FP8_MAX = 448.0
FP8_MIN_NORMAL = 2.0 ** -6
ROUNDER = 1.5 * 2.0 ** 20
HUGE = 3.0e38
Q8_STEPS = 8
QC = D * F // P // UNITS

ST, VG0, QT, VG1, KTJ, VG2, VG3 = range(7)
JOBS = 7


def gsa_swiglu(nc, x, Wq, Wk, Wv, Wg, Ws, Wo, gnorm, gate_w, up_w, down_w, gate_s, up_s, down_s, out):
    fp8_scratch = nc.dram_tensor("fp8_weights", (3, P, D * F // P), F32, kind="Internal").ap()
    flat = [w.rearrange("a b -> (a b)").rearrange("(p c) -> p c", p=P) for w in (gate_w, up_w, down_w)]

    top = ExitStack()
    with top:
        def sb(name, shape, dt=F32, ctx=top):
            return ctx.enter_context(nc.sbuf_tensor(name, shape, dt))

        def sem(name):
            return top.enter_context(nc.semaphore(name))

        y = sb("y", [P, TILES, D])
        ident = sb("ident", [P, P])
        bank = [top.enter_context(nc.psum_tensor(f"bank{i}", [P, 512], F32)) for i in range(8)]

        s_const = sem("const_ready")
        s_x = [sem(f"x_loaded{b}") for b in range(B)]
        s_fp8_out = sem("fp8_stored")
        attention(nc, sb, sem, x, Wq, Wk, Wv, Wg, Ws, Wo, gnorm, flat, fp8_scratch, y, ident, bank,
                  s_const, s_x, s_fp8_out)
        feed_forward(nc, sb, sem, fp8_scratch, gate_s, up_s, down_s, out, y, ident, bank)


def attention(nc, sb_top, sem, x, Wq, Wk, Wv, Wg, Ws, Wo, gnorm, flat, fp8_scratch, y, ident, bank,
              s_const, s_x, s_fp8_out):
    PJ, A, (T0, T1, T2, T3) = bank[0:2], bank[2:4], bank[4:8]

    with ExitStack() as ctx:
        def sb(name, shape, dt=F32):
            return sb_top(name, shape, dt, ctx)

        xh, xl = (sb(n, [P, KT, B * T], F32R) for n in ("xT_hi", "xT_lo"))
        wh = {n: sb(f"w{n}_hi", [P, KT, P], F32R) for n in "sqk"}
        wl = {n: sb(f"w{n}_lo", [P, KT, P], F32R) for n in "sqk"}
        vgh, vgl = (sb(n, [P, KT, 2 * 2 * DV], F32R) for n in ("wvg_hi", "wvg_lo"))
        woh, wol = (sb(n, [P, 2, D], F32R) for n in ("wo_hi", "wo_lo"))
        stage = sb("stage", [P, D])
        stage_vg = sb("stage_vg", [P, KT, 4 * DV])

        qT, kT = sb("qT", [P, T]), sb("kT", [P, T])
        k_tok, e_tok, c_inv = (sb(n, [P, CH, P]) for n in ("k_tok", "e_tok", "c_inv"))
        eT = [sb(f"eT{i}", [P, T]) for i in range(2)]
        cT = [sb(f"cT{i}", [P, T]) for i in range(2)]
        v = [sb(f"v{i}", [P, CH, 2 * DV]) for i in range(2)]
        g = [sb(f"g{i}", [P, CH, 2 * DV]) for i in range(2)]
        th = sb("tanh_half_g", [P, 2 * DV])
        aT = sb("aT", [P, 2, CH, P])
        hk = sb("hk", [P, CH - 1, P])
        hv = sb("hv", [P, CH - 1, 2 * DV])
        p = sb("p", [P, CH * P])
        wT = sb("wT", [P, T])
        o = sb("o", [P, CH, 2 * DV])
        oh, ol = (sb(n, [P, 2, T], F32R) for n in ("oT_hi", "oT_lo"))
        q8 = sb("q8", [P, 3, QC])
        q8t = sb("q8t", [P, 3, QC])
        tri = sb("tri", [P, P])
        half_gn = sb("half_gn", [P, 1])
        neg_half = sb("neg_half", [P, 2 * CH])
        ssq, rstd = sb("ssq", [P, 2 * CH]), sb("rstd", [P, 2 * CH])
        mx, sm, rs = (sb(n, [P, 2 * CH]) for n in ("slot_max", "slot_sum", "slot_rsum"))
        stats = q8[:, 0, 0:TILES * 6].rearrange("p (t s) -> p t s", s=6)
        mv = q8t[:, 0, 0:TILES * 2].rearrange("p (t s) -> p t s", s=2)
        sd = q8t[:, 1, 0:TILES]

        s_gn = sem("gnorm_loaded")
        s_ln = sem("ln_step")
        s_mv = sem("ln_stats_step")
        s_sd = sem("ln_sd_ready")
        s_zero, s_gnh = sem("states_zeroed"), sem("half_gnorm_ready")
        s_xn = sem("ln_x_ready")
        s_xtr = sem("ln_x_transposed")
        s_xh, s_xl = sem("xT_hi_ready"), sem("xT_lo_ready")
        s_stage, s_stage_vg = sem("stage_loaded"), [sem(f"stage_vg_loaded{k}") for k in range(KT)]
        s_wh, s_wl = sem("w_hi_ready"), sem("w_lo_ready")
        s_vgh = sem("vg_hi_ready")
        s_vgl, s_vgl2 = sem("vg_lo_ready"), sem("vg_lo_2_ready")
        s_wos = sem("wo_scaled")
        s_job = sem("job_done")
        s_clip, s_q, s_k, s_e = sem("s_clipped"), sem("q_ready"), sem("k_ready"), sem("e_ready")
        s_scan, s_cinv = sem("c_summed"), sem("c_inverted")
        s_v, s_th, s_g = sem("v_ready"), sem("tanh_ready"), sem("g_ready")
        s_trk, s_tre, s_trc = sem("k_transposed"), sem("e_transposed"), sem("c_transposed")
        s_ktok, s_etok, s_ctok = sem("k_tok_ready"), sem("e_tok_ready"), sem("c_inv_ready")
        s_a, s_am = sem("scores_done"), sem("scores_masked")
        s_hkd, s_hk = sem("hk_parts_done"), sem("hk_step")
        s_hvd, s_hv = sem("hv_parts_done"), sem("hv_step")
        s_ok, s_okn = sem("ok_done"), sem("softmax_step")
        s_exp = sem("slot_exp_ready")
        s_trw, s_wT = sem("w_transposed"), sem("wT_ready")
        s_b, s_bm = sem("value_weights_done"), sem("value_weights_masked")
        s_o, s_ocp, s_sq = sem("o_done"), sem("o_copied"), sem("o_squared")
        s_ms, s_rstd, s_og = sem("o_mean_square"), sem("o_rstd_ready"), sem("o_gated")
        s_tro, s_oh, s_ol = sem("o_transposed"), sem("oT_hi_ready"), sem("oT_lo_ready")
        s_y, s_ya = sem("y_done"), sem("y_added")
        s_q8in, s_q8 = sem("fp8_in_loaded"), sem("fp8_step")

        block = ctx.enter_context(nc.Block())

        def split_next(i, tail):
            return i == 2 and not tail, i in (0, B)

        @block.sync
        def _(sp):
            for b in range(B):
                sp.dma_start(y[:, CH * b:CH * (b + 1), :],
                             x[b].rearrange("(c p) d -> p c d", p=P)).then_inc(s_x[b], 16)
            sp.dma_start(half_gn[:, :], gnorm.rearrange("(p a) -> p a", a=1)).then_inc(s_gn, 16)

            def load_sqk(pair, n):
                if not (isinstance(pair, int) and n == 0):
                    sp.wait_ge(s_wl, pair * 5 + n)
                sp.dma_start(stage[:, :].rearrange("p (k n) -> p k n", k=KT),
                             (Ws, Wq, Wk)[n].rearrange("(k p) n -> p k n", p=P)[:, :, bass.ds(pair * P, P)]
                             ).then_inc(s_stage, 16)

            def load_vg(pair):
                for k in range(KT):
                    if not isinstance(pair, int):
                        sp.wait_ge((s_vgl, s_vgl2)[k // 2], (pair - 1) * 2 + k % 2 + 1)
                    for n, w in enumerate((Wv, Wg)):
                        sp.dma_start(stage_vg[:, k, n * 2 * DV:(n + 1) * 2 * DV],
                                     w[P * k:P * (k + 1), bass.ds(pair * 2 * DV, 2 * DV)]
                                     ).then_inc(s_stage_vg[k], 16)

            def load_o(pair, a):
                sp.wait_ge(s_wl, pair * 5 + 3 + a)
                sp.dma_start(stage[:, :], Wo[bass.ds(pair * 2 * DV + a * DV, DV), :]).then_inc(s_stage, 16)

            def load_q8(u):
                if isinstance(u, int) and u == 0:
                    sp.wait_ge(s_xn, TILES)
                else:
                    sp.wait_ge(s_fp8_out, 16 * u)
                for n, w in enumerate(flat):
                    sp.dma_start(q8[:, n, :], w[:, bass.ds(u * QC, QC)]).then_inc(s_q8in, 16)

            def store_q8(u):
                sp.wait_ge(s_q8, Q8_STEPS * (u + 1))
                sp.dma_start(fp8_scratch[:, :, bass.ds(u * QC, QC)].rearrange("n p c -> p n c"),
                             q8[:, :, :]).then_inc(s_fp8_out, 16)

            load_sqk(0, 0)
            load_vg(0)
            load_sqk(0, 1)
            load_sqk(0, 2)
            load_o(0, 0)
            load_q8(0)
            load_o(0, 1)
            store_q8(0)
            with sp.Fori(0, PAIRS - 1) as h:
                for i in range(1, B + 1):
                    load_q8(h * B + i)
                    if i == 1:
                        load_sqk(h + 1, 0)
                        load_vg(h + 1)
                    if i == 2:
                        load_sqk(h + 1, 1)
                        load_sqk(h + 1, 2)
                        load_o(h + 1, 0)
                    if i == B:
                        load_o(h + 1, 1)
                    store_q8(h * B + i)
            for u in range(UNITS - B + 1, UNITS):
                load_q8(u)
                store_q8(u)
            sp.wait_ge(s_fp8_out, 16 * UNITS)

        @block.tensor
        def _(pe):
            def product3(dst, pairs):
                n = len(pairs)
                for k, (w_hi, w_lo, m_hi, m_lo) in enumerate(pairs):
                    pe.matmul(dst, w_hi, m_hi, start=(k == 0), stop=False)
                    pe.matmul(dst, w_hi, m_lo, start=False, stop=False)
                    last = pe.matmul(dst, w_lo, m_hi, start=False, stop=(k == n - 1))
                return last

            def job(j, u, i):
                b = i % B
                dst = PJ[(JOBS * i + j) % 2]
                first = isinstance(u, int) and u == 0
                if j == ST:
                    if not first:
                        pe.wait_ge(s_v, u * CH - 1)
                        pe.wait_ge(s_g, u * CH - 1)
                    if b == 0:
                        pe.wait_ge(s_wl, 5 * pair_of(u, i) + 1)
                    if not isinstance(u, int) or u < B:
                        pe.wait_ge(s_xl, CH * (b + 1))
                elif j == VG0:
                    if not first:
                        pe.wait_ge(s_v, u * CH)
                        pe.wait_ge(s_g, u * CH)
                    if b == 0:
                        pe.wait_ge(s_vgl, 2 * pair_of(u, i) + 2)
                        pe.wait_ge(s_vgl2, 2 * pair_of(u, i) + 2)
                elif j == QT:
                    pe.wait_ge(s_clip, u + 1)
                    if b == 0:
                        pe.wait_ge(s_wl, 5 * pair_of(u, i) + 2)
                elif j == VG1:
                    pe.wait_ge(s_v, u * CH + 1)
                    pe.wait_ge(s_g, u * CH + 1)
                elif j == KTJ:
                    pe.wait_ge(s_q, u + 1)
                    if b == 0:
                        pe.wait_ge(s_wl, 5 * pair_of(u, i) + 3)
                elif j == VG2:
                    pe.wait_ge(s_v, u * CH + 2)
                    pe.wait_ge(s_g, u * CH + 2)
                elif j == VG3:
                    pe.wait_ge(s_k, u + 1)
                if j in (ST, QT, KTJ):
                    n = {ST: "s", QT: "q", KTJ: "k"}[j]
                    cols = slice(T * b, T * (b + 1))
                    last = product3(dst[:, :], [(wh[n][:, k, :], wl[n][:, k, :], xh[:, k, cols], xl[:, k, cols])
                                                for k in range(KT)])
                else:
                    c = {VG0: 0, VG1: 1, VG2: 2, VG3: 3}[j]
                    cols = slice(T * b + P * c, T * b + P * (c + 1))
                    last = product3(dst[:, :], [(xh[:, k, cols], xl[:, k, cols], vgh[:, k, :], vgl[:, k, :])
                                                for k in range(KT)])
                last.then_inc(s_job, 1)

            def pair_of(u, i):
                return u // B if isinstance(u, int) else pair_reg[0] + i // B

            pair_reg = [None]

            def out_transposes(u):
                pe.wait_ge(s_og, u + 1)
                pe.wait_ge(s_am, 2 * (u + 1) + 2) if not last_tail[0] else pe.wait_ge(s_bm, 2 * (u + 1))
                for a in range(2):
                    for c in range(CH):
                        last = pe.transpose(A[a][:, c * P:(c + 1) * P], o[:, c, a * DV:(a + 1) * DV], ident[:, :])
                    last.then_inc(s_tro, 1)

            def out_product(u, pair_ready):
                pe.wait_ge(s_oh, 2 * (u + 1))
                pe.wait_ge(s_ol, 2 * (u + 1))
                if pair_ready is not None:
                    pe.wait_ge(s_wl, pair_ready)
                for c, dst in enumerate((T2, A[0], A[1], T0)):
                    if c == 3:
                        pe.wait_ge(s_okn, 6 * (u + 1) + 1 if not last_tail[0] else 6 * (u + 1))
                    cols = slice(c * P, (c + 1) * P)
                    product3(dst[:, :], [(oh[:, a, cols], ol[:, a, cols], woh[:, a, :], wol[:, a, :])
                                         for a in range(2)]).then_inc(s_y, 1)

            last_tail = [False]

            def unit(u, i, last=False, tail=False):
                par = i % 2
                first = isinstance(u, int) and u == 0
                nu, ni = u + 1, i + 1
                pe.wait_ge(s_k, u + 1)
                if not first:
                    pe.wait_ge(s_okn, 6 * (u - 1) + 1)
                for c in range(CH):
                    mm = pe.transpose(T0[:, c * P:(c + 1) * P], kT[:, c * P:(c + 1) * P], ident[:, :])
                mm.then_inc(s_trk, 1)
                pe.wait_ge(s_q, u + 1)
                if not first:
                    pe.wait_ge(s_bm, 2 * u)
                for c in range(CH):
                    for a in range(2):
                        hs, cs = slice(DK * a, DK * (a + 1)), slice(c * P, (c + 1) * P)
                        mm = pe.matmul(A[a][:, cs], kT[hs, cs], qT[hs, cs], start=True, stop=True)
                mm.then_inc(s_a, 1)
                pe.wait_ge(s_e, u + 1)
                if not first:
                    pe.wait_ge(s_sq, 2 * CH * u)
                for c in range(CH):
                    mm = pe.transpose(T1[:, c * P:(c + 1) * P], eT[par][:, c * P:(c + 1) * P], ident[:, :])
                mm.then_inc(s_tre, 1)
                pe.wait_ge(s_cinv, u + 1)
                if not first:
                    pe.wait_ge(s_wT, u)
                for c in range(CH):
                    mm = pe.transpose(T2[:, c * P:(c + 1) * P], cT[par][:, c * P:(c + 1) * P], ident[:, :])
                mm.then_inc(s_trc, 1)
                if not last:
                    job(ST, nu, ni)
                pe.wait_ge(s_ktok, u + 1)
                pe.wait_ge(s_etok, u + 1)
                for c in range(CH - 1):
                    mm = pe.matmul(T3[:, c * P:(c + 1) * P], k_tok[:, c, :], e_tok[:, c, :], start=True, stop=True)
                mm.then_inc(s_hkd, 1)
                if not last:
                    job(VG0, nu, ni)
                pe.wait_ge(s_am, 2 * u + 2)
                pe.wait_ge(s_hk, 3 * (u + 1))
                for c in range(CH):
                    if c:
                        pe.matmul(T0[:, c * P:(c + 1) * P], qT[:, c * P:(c + 1) * P], hk[:, c - 1, :],
                                  start=False, stop=False, skip_group_check=True)
                    for a in range(2):
                        mm = pe.matmul(T0[:, c * P + a * M:c * P + (a + 1) * M], aT[:, a, c, :],
                                       e_tok[:, c, a * M:(a + 1) * M], start=(c == 0 and a == 0),
                                       stop=(c == CH - 1 and a == 1), skip_group_check=True)
                mm.then_inc(s_ok, 1)
                pe.wait_ge(s_v, (u + 1) * CH)
                for c in range(CH - 1):
                    dst = (T1[:, 0:256], T1[:, 256:512], T3[:, 0:256])[c]
                    mm = pe.matmul(dst, e_tok[:, c, :], v[par][:, c, :], start=True, stop=True)
                mm.then_inc(s_hvd, 1)
                if not first:
                    out_transposes(u - 1)
                if not last:
                    job(QT, nu, ni)
                if not first:
                    pe.wait_ge(s_ctok, u + 1)
                    out_product(u - 1, wo_ready(u, i))
                pe.wait_ge(s_okn, 6 * (u + 1))
                if not first:
                    pe.wait_ge(s_ya, u * CH - 3)
                for c in range(CH):
                    mm = pe.transpose(T2[:, c * P:(c + 1) * P], p[:, c * P:(c + 1) * P], ident[:, :])
                mm.then_inc(s_trw, 1)
                if not last:
                    job(VG1, nu, ni)
                    job(KTJ, nu, ni)
                pe.wait_ge(s_wT, u + 1)
                if not first:
                    pe.wait_ge(s_ya, u * CH)
                for c in range(CH):
                    for a in range(2):
                        hs, cs = slice(M * a, M * (a + 1)), slice(c * P, (c + 1) * P)
                        mm = pe.matmul(A[a][:, cs], eT[par][hs, cs], wT[hs, cs], start=True, stop=True)
                mm.then_inc(s_b, 1)
                if not last:
                    job(VG2, nu, ni)
                pe.wait_ge(s_bm, 2 * (u + 1))
                pe.wait_ge(s_hv, 3 * (u + 1))
                for c in range(CH):
                    bk, at = (T1, T3)[c // 2], (c % 2) * 2 * DV
                    if c:
                        mm = pe.matmul(bk[:, at:at + 2 * DV], wT[:, c * P:(c + 1) * P], hv[:, c - 1, :],
                                       start=(c == 2), stop=False, skip_group_check=True)
                    for a in range(2):
                        mm = pe.matmul(bk[:, at + a * DV:at + (a + 1) * DV], aT[:, a, c, :],
                                       v[par][:, c, a * DV:(a + 1) * DV], start=(c == 0 and a == 0),
                                       stop=(a == 1 and c % 2 == 1), skip_group_check=True)
                    if c % 2:
                        mm.then_inc(s_o, 1)
                if not last:
                    job(VG3, nu, ni)

            def wo_ready(u, i):
                if i % B != 1:
                    return None
                return 5 * (u // B if isinstance(u, int) else pair_reg[0]) + 5

            pe.wait_ge(s_const, 4)
            for t in range(TILES):
                pe.wait_ge(s_xn, t + 1)
                if t >= 2:
                    pe.wait_ge(s_xl, t - 1)
                for k in range(KT):
                    mm = pe.transpose((T0, T1)[t % 2][:, k * P:(k + 1) * P],
                                      o[:, 2 * (t % 2):2 * (t % 2) + 2, :].rearrange("p a d -> p (a d)")
                                      [:, k * P:(k + 1) * P], ident[:, :])
                mm.then_inc(s_xtr, 1)
            for j in range(JOBS):
                job(j, 0, 0)
            pe.wait_ge(s_xl, TILES)
            unit(0, 0)
            with pe.Fori(0, PAIRS - 1) as h:
                pair_reg[0] = h
                for i in range(1, B + 1):
                    unit(h * B + i, i)
            for i in range(1, B):
                unit((PAIRS - 1) * B + i, i, last=(i == B - 1))
            last_tail[0] = True
            out_transposes(UNITS - 1)
            out_product(UNITS - 1, None)

        @block.scalar
        def _(act):
            def copy(dst, src):
                return act.activation(dst, src, ACT.Copy)

            def split_w(n, dst, count):
                act.wait_ge(s_stage, 16 * count)
                copy(dst, stage[:, :].rearrange("p (k n) -> p k n", k=KT)).then_inc(s_wh, 1)

            def split_next_w(n, j, nu):
                act.wait_ge(s_job, nu * JOBS + j + 1)
                split_w(n, wh["sqk"[n]][:, :, :], (h_of[0] + 1) * 5 + n + 1)

            def split_vg(pair, k):
                act.wait_ge(s_stage_vg[k], (pair + 1) * 32)
                copy(vgh[:, k, :], stage_vg[:, k, :]).then_inc(s_vgh, 1)

            def split_o(pair, a):
                act.wait_ge(s_stage, (pair * 5 + 4 + a) * 16)
                act.activation(stage[:, :], stage[:, :], ACT.Copy, scale=half_gn[:, 0:1]).then_inc(s_wos, 1)
                act.wait_ge(s_wos, pair * 2 + a + 1)
                copy(woh[:, a, :], stage[:, :]).then_inc(s_wh, 1)

            def evac(j, u, i):
                par = i % 2
                src = PJ[(JOBS * i + j) % 2]
                first = isinstance(u, int) and u == 0
                if j == ST:
                    act.wait_ge(s_clip, u + 1)
                    act.activation(eT[par][:, :], eT[par][:, :], ACT.Exp).then_inc(s_e, 1)
                    return
                act.wait_ge(s_job, u * JOBS + j + 1)
                if j == QT:
                    if not first:
                        act.wait_ge(s_ok, u)
                    copy(qT[:, :], src[:, :]).then_inc(s_q, 1)
                elif j == KTJ:
                    if not first:
                        act.wait_ge(s_a, u)
                    copy(kT[:, :], src[:, :]).then_inc(s_k, 1)
                else:
                    c = {VG0: 0, VG1: 1, VG2: 2, VG3: 3}[j]
                    if not isinstance(u, int) or u >= 2:
                        act.wait_ge(s_o, 2 * (u - 1))
                    copy(v[par][:, c, :], src[:, 0:2 * DV]).then_inc(s_v, 1)
                    if not (first and c == 0):
                        act.wait_ge(s_g, u * CH + c)
                    act.activation(th[:, :], src[:, 2 * DV:4 * DV], ACT.Tanh, scale=0.5).then_inc(s_th, 1)

            def out_hi(u):
                for a in range(2):
                    act.wait_ge(s_tro, 2 * u + a + 1)
                    if a == 0 and not (isinstance(u, int) and u == 0):
                        act.wait_ge(s_y, CH * u)
                    copy(oh[:, a, :], A[a][:, :]).then_inc(s_oh, 1)

            def unit(u, i, last=False, tail=False):
                first = isinstance(u, int) and u == 0
                nu, ni = u + 1, i + 1
                act.wait_ge(s_trk, u + 1)
                if not first:
                    act.wait_ge(s_hkd, u)
                copy(k_tok[:, :, :].rearrange("p c m -> p (c m)"), T0[:, :]).then_inc(s_ktok, 1)
                if i == 3 and not tail:
                    act.wait_ge(s_job, u * JOBS + VG3 + 1)
                    for k in range(KT):
                        split_vg(h_of[0] + 1, k)
                act.wait_ge(s_tre, u + 1)
                if not first:
                    act.wait_ge(s_hvd, u)
                copy(e_tok[:, :, :].rearrange("p c m -> p (c m)"), T1[:, :]).then_inc(s_etok, 1)
                act.wait_ge(s_trc, u + 1)
                if not first:
                    act.wait_ge(s_okn, 6 * (u - 1) + 1)
                copy(c_inv[:, :, :].rearrange("p c m -> p (c m)"), T2[:, :]).then_inc(s_ctok, 1)
                if not last:
                    evac(ST, nu, ni)
                projections, outputs = split_next(i, tail)
                if not last:
                    evac(VG0, nu, ni)
                if not first:
                    out_hi(u - 1)
                act.wait_ge(s_okn, 6 * u + 3)
                act.activation(p[:, :], p[:, :], ACT.Exp).then_inc(s_exp, 1)
                if projections:
                    split_next_w(0, ST, nu)
                if not last:
                    evac(QT, nu, ni)
                    evac(VG1, nu, ni)
                if projections:
                    split_next_w(1, QT, nu)
                if outputs:
                    if not first:
                        act.wait_ge(s_y, CH * u)
                    split_o(0 if first else h_of[0] + 1, 0)
                if not last:
                    evac(KTJ, nu, ni)
                if projections:
                    split_next_w(2, KTJ, nu)
                if not last:
                    evac(VG2, nu, ni)
                if outputs:
                    split_o(0 if first else h_of[0] + 1, 1)
                if not first:
                    act.wait_ge(s_tro, 2 * u)
                    act.wait_ge(s_rstd, u)
                for k in range(2):
                    act.wait_ge(s_o, 2 * u + k + 1)
                    copy(o[:, 2 * k:2 * k + 2, :].rearrange("p a d -> p (a d)"), (T1, T3)[k][:, :]
                         ).then_inc(s_ocp, 1)
                    act.wait_ge(s_ocp, 2 * u + k + 1)
                    for c in (2 * k, 2 * k + 1):
                        for a in range(2):
                            at = (c % 2) * 2 * DV + a * DV
                            head = (T1, T3)[k][:, at:at + DV]
                            act.activation(head, head, ACT.Square,
                                           accum_out=ssq[:, 2 * c + a:2 * c + a + 1]).then_inc(s_sq, 1)
                if not last:
                    evac(VG3, nu, ni)

            h_of = [0]
            for t in range(-1, TILES):
                if t % CH == CH - 1 and t < TILES - 1:
                    b = (t + 1) // CH
                    act.wait_ge(s_ln, b + 1)
                    act.activation(sd[:, CH * b:CH * (b + 1)], sd[:, CH * b:CH * (b + 1)], ACT.Sqrt
                                   ).then_inc(s_sd, 1)
                if t >= 0:
                    act.wait_ge(s_xtr, t + 1)
                    copy(xh[:, :, t * P:(t + 1) * P],
                         (T0, T1)[t % 2][:, :].rearrange("p (k t) -> p k t", k=KT)).then_inc(s_xh, 1)
            for n in range(3):
                split_w(n, wh["sqk"[n]][:, :, :], n + 1)
            for k in range(KT):
                split_vg(0, k)
            act.wait_ge(s_gn, 16)
            act.mul(half_gn[:, :], half_gn[:, :], 0.5).then_inc(s_gnh, 1)
            for j in range(JOBS):
                evac(j, 0, 0)
            act.wait_ge(s_gnh, 1)
            unit(0, 0)
            with act.Fori(0, PAIRS - 1) as h:
                h_of[0] = h
                for i in range(1, B + 1):
                    unit(h * B + i, i)
            for i in range(1, B):
                unit((PAIRS - 1) * B + i, i, last=(i == B - 1), tail=True)
            out_hi(UNITS - 1)

        @block.gpsimd
        def _(pool):
            pool.memset(ident[:, :], 1.0).then_inc(s_const, 1)
            pool.wait_ge(s_const, 1)
            pool.affine_select(out=ident[:, :], in_=ident[:, :], compare_op=ALU.is_equal, fill=0.0, base=0,
                               pattern=[[1, P]], channel_multiplier=-1).then_inc(s_const, 1)
            pool.memset(tri[:, :], 1.0).then_inc(s_const, 1)
            pool.memset(neg_half[:, :], -0.5)
            pool.wait_ge(s_const, 3)
            pool.affine_select(out=tri[:, :], in_=tri[:, :], compare_op=ALU.is_ge, fill=0.0, base=0,
                               pattern=[[1, P]], channel_multiplier=-1).then_inc(s_const, 1)

            def lo(n, w_lo, w_hi, w):
                pool.wait_ge(s_wh, n)
                pool.tensor_tensor(w_lo, w, w_hi.bitcast(F32), ALU.subtract).then_inc(s_wl, 1)

            def lo_w(n, pair):
                name = "sqk"[n]
                lo(pair * 5 + n + 1, wl[name][:, :, :], wh[name][:, :, :],
                   stage[:, :].rearrange("p (k n) -> p k n", k=KT))

            def lo_vg(pair, k):
                pool.wait_ge(s_vgh, pair * KT + k + 1)
                pool.tensor_tensor(vgl[:, k, :], stage_vg[:, k, :], vgh[:, k, :].bitcast(F32), ALU.subtract
                                   ).then_inc(s_vgl2, 1)

            def unit(u, i, last=False, tail=False):
                projections, outputs = split_next(i, tail)
                first = isinstance(u, int) and u == 0
                if not first:
                    rsqrt(u - 1)
                if i == 3 and not tail:
                    pool.wait_ge(s_job, u * JOBS + VG3 + 1)
                    for k in range(2, KT):
                        lo_vg(h_of[0] + 1, k)
                if projections:
                    for n in range(3):
                        lo_w(n, h_of[0] + 1)
                if outputs:
                    pair = 0 if first else h_of[0] + 1
                    for a in range(2):
                        if not first:
                            pool.wait_ge(s_y, CH * u)
                        lo(pair * 5 + 4 + a, wol[:, a, :], woh[:, a, :], stage[:, :])

            def rsqrt(u):
                pool.wait_ge(s_ms, u + 1)
                if not (isinstance(u, int) and u == 0):
                    pool.wait_ge(s_og, u)
                pool.tensor_tensor(rstd[:, :], ssq[:, :], neg_half[:, :], ALU.pow).then_inc(s_rstd, 1)

            h_of = [0]
            for n in range(3):
                lo_w(n, 0)
            for k in range(2, KT):
                lo_vg(0, k)
            unit(0, 0)
            with pool.Fori(0, PAIRS - 1) as h:
                h_of[0] = h
                for i in range(1, B + 1):
                    unit(h * B + i, i)
            for i in range(1, B):
                unit((PAIRS - 1) * B + i, i, last=(i == B - 1), tail=True)
            rsqrt(UNITS - 1)

        @block.vector
        def _(dve):
            tri4 = tri[:, :].rearrange("p (c t) -> p c t", c=1).broadcast_to([P, CH, P])

            def lo(dst, src, hi):
                return dve.tensor_tensor(dst, src, hi.bitcast(F32), ALU.subtract)

            def lo_vg(pair, k):
                dve.wait_ge(s_vgh, pair * KT + k + 1)
                lo(vgl[:, k, :], stage_vg[:, k, :], vgh[:, k, :]).then_inc(s_vgl, 1)

            def clip(u, i):
                dve.wait_ge(s_job, u * JOBS + ST + 1)
                if not isinstance(u, int) or u >= 2:
                    dve.wait_ge(s_b, u - 1)
                dve.tensor_scalar(eT[i % 2][:, :], PJ[(JOBS * i + ST) % 2][:, :], -CLAMP, CLAMP,
                                  ALU.max, ALU.min).then_inc(s_clip, 1)

            def sums(u, i):
                dve.wait_ge(s_e, u + 1)
                if not isinstance(u, int) or u >= 2:
                    dve.wait_ge(s_trc, u - 1)
                dve.tensor_tensor_scan(cT[i % 2][:, :], eT[i % 2][:, :], eT[i % 2][:, :], 0.0, ALU.add,
                                       ALU.bypass).then_inc(s_scan, 1)
                dve.wait_ge(s_scan, u + 1)
                dve.reciprocal(cT[i % 2][:, :], cT[i % 2][:, :]).then_inc(s_cinv, 1)

            def gate(c, u, i):
                if not isinstance(u, int) or u >= 2:
                    dve.wait_ge(s_og, u - 1)
                dve.wait_ge(s_th, u * CH + c + 1)
                dve.scalar_tensor_tensor(out=g[i % 2][:, c, :], in0=th[:, :], scalar=1.0,
                                         in1=PJ[(JOBS * i + (VG0, VG1, VG2, VG3)[c]) % 2][:, 2 * DV:4 * DV],
                                         op0=ALU.add, op1=ALU.mult).then_inc(s_g, 1)

            def mask(u, s_in, s_out, used, count):
                dve.wait_ge(s_in, u + 1)
                if count is not None:
                    dve.wait_ge(used, count)
                for a in range(2):
                    dve.tensor_tensor(aT[:, a, :, :], A[a][:, :].rearrange("p (c t) -> p c t", c=CH), tri4,
                                      ALU.mult).then_inc(s_out, 1)

            def states(u, dst, width, parts, s_step):
                for c in range(CH - 1):
                    if c:
                        dve.wait_ge(s_step, u * 3 + c)
                    for a in range(2):
                        rows, cols = slice(64 * a, 64 * (a + 1)), slice(width * a, width * (a + 1))
                        src = parts(c)[rows, cols]
                        if c == 0:
                            st = dve.tensor_copy(dst[rows, c, cols], src)
                        else:
                            st = dve.tensor_tensor(dst[rows, c, cols], src, dst[rows, c - 1, cols], ALU.add)
                    st.then_inc(s_step, 1)

            def mean_square(u):
                dve.wait_ge(s_sq, 8 * (u + 1))
                dve.tensor_scalar(ssq[:, :], ssq[:, :], 1.0 / DV, EPS, ALU.mult, ALU.add).then_inc(s_ms, 1)

            def norm_gate(u, i):
                dve.wait_ge(s_rstd, u + 1)
                for c in range(CH):
                    for a in range(2):
                        blk = o[:, c, a * DV:(a + 1) * DV]
                        st = dve.scalar_tensor_tensor(out=blk, in0=blk, scalar=rstd[:, 2 * c + a:2 * c + a + 1],
                                                      in1=g[i % 2][:, c, a * DV:(a + 1) * DV],
                                                      op0=ALU.mult, op1=ALU.mult)
                st.then_inc(s_og, 1)

            def out_lo(u):
                for a in range(2):
                    dve.wait_ge(s_oh, 2 * u + a + 1)
                    if a == 0 and not (isinstance(u, int) and u == 0):
                        dve.wait_ge(s_y, CH * u)
                    lo(ol[:, a, :], A[a][:, :], oh[:, a, :]).then_inc(s_ol, 1)

            def add_y(u, i, c):
                dve.wait_ge(s_y, CH * u + c + 1)
                t = CH * (i % B) + c
                dve.tensor_tensor(y[:, t, :], y[:, t, :], (T2, A[0], A[1], T0)[c][:, :], ALU.add
                                  ).then_inc(s_ya, 1)

            def quantise(u, steps):
                w, t = (q[:, :, :].rearrange("p a b -> p (a b)") for q in (q8, q8t))
                todo = (
                    lambda: dve.tensor_scalar(t.bitcast(I32), w.bitcast(I32), 0x7F800000, None, ALU.bitwise_and),
                    lambda: dve.tensor_scalar(t, t, FP8_MIN_NORMAL, ROUNDER, ALU.max, ALU.mult),
                    lambda: dve.tensor_tensor(w, w, t, ALU.add),
                    lambda: dve.tensor_tensor(w, w, t, ALU.subtract),
                    lambda: dve.tensor_tensor(t, w, w, ALU.mult),
                    lambda: dve.tensor_scalar(t, t, FP8_MAX ** 2, FP8_MAX ** 2, ALU.max, ALU.subtract),
                    lambda: dve.tensor_scalar(t, t, HUGE, HUGE, ALU.mult, ALU.mult),
                    lambda: dve.scalar_tensor_tensor(out=w, in0=t, scalar=0.0, in1=w, op0=ALU.mult, op1=ALU.add))
                for n in range(Q8_STEPS)[steps]:
                    if n == 0:
                        dve.wait_ge(s_q8in, (u + 1) * 48)
                    else:
                        dve.wait_ge(s_q8, u * Q8_STEPS + n)
                    todo[n]().then_inc(s_q8, 1)

            def unit(u, i, last=False, tail=False):
                first = isinstance(u, int) and u == 0
                nu, ni = u + 1, i + 1
                if i == 3 and not tail:
                    dve.wait_ge(s_job, u * JOBS + VG3 + 1)
                    for k in range(2):
                        lo_vg(h_of[0] + 1, k)
                mask(u, s_a, s_am, s_o, None if first else 2 * u)
                if not first:
                    norm_gate(u - 1, i - 1)
                if not last:
                    clip(nu, ni)
                dve.wait_ge(s_hkd, u + 1)
                if not first:
                    dve.wait_ge(s_ok, u)
                states(u, hk, DK, lambda c: T3[:, c * P:(c + 1) * P], s_hk)
                if not last:
                    sums(nu, ni)
                    gate(0, nu, ni)
                k = [6 * u]

                def step(ins, wait=True):
                    k[0] += 1
                    ins.then_inc(s_okn, 1)
                    if wait:
                        dve.wait_ge(s_okn, k[0])

                p3 = p[:, :].rearrange("p (s m) -> p s m", m=M)
                dve.wait_ge(s_ok, u + 1)
                dve.wait_ge(s_ctok, u + 1)
                if not first:
                    dve.wait_ge(s_trw, u)
                step(dve.scalar_tensor_tensor(out=p[:, :], in0=T0[:, :], scalar=SCALE,
                                              in1=c_inv[:, :, :].rearrange("p c m -> p (c m)"),
                                              op0=ALU.mult, op1=ALU.mult))
                step(dve.tensor_reduce(mx[:, :], p3, AX.X, ALU.max))
                step(dve.tensor_tensor(p3, p3, mx[:, :].rearrange("p (s a) -> p s a", a=1).broadcast_to(
                    [P, 2 * CH, M]), ALU.subtract), wait=False)
                if not first:
                    out_lo(u - 1)
                dve.wait_ge(s_hvd, u + 1)
                if not first:
                    dve.wait_ge(s_o, 2 * u)
                states(u, hv, DV, lambda c: (T1[:, 0:256], T1[:, 256:512], T3[:, 0:256])[c], s_hv)
                dve.wait_ge(s_exp, u + 1)
                step(dve.tensor_reduce(sm[:, :], p3, AX.X, ALU.add))
                step(dve.reciprocal(rs[:, :], sm[:, :]))
                step(dve.tensor_tensor(p3, p3, rs[:, :].rearrange("p (s a) -> p s a", a=1).broadcast_to(
                    [P, 2 * CH, M]), ALU.mult), wait=False)
                if not first:
                    for c in range(CH):
                        add_y(u - 1, i - 1, c)
                dve.wait_ge(s_trw, u + 1)
                if not first:
                    dve.wait_ge(s_o, 2 * u)
                dve.tensor_tensor(wT[:, :], T2[:, :], cT[i % 2][:, :], ALU.mult).then_inc(s_wT, 1)
                if not last:
                    gate(1, nu, ni)
                quantise(u, slice(0, 5))
                mask(u, s_b, s_bm, s_ok, u + 1)
                quantise(u, slice(5, Q8_STEPS))
                if not last:
                    gate(2, nu, ni)
                mean_square(u)
                if not last:
                    gate(3, nu, ni)

            h_of = [0]
            dve.memset(hk[:, :, :], 0.0)
            dve.memset(hv[:, :, :], 0.0).then_inc(s_zero, 1)
            dve.wait_ge(s_zero, 1)

            def x_lo(t):
                dve.wait_ge(s_xh, t + 1)
                lo(xl[:, :, t * P:(t + 1) * P], (T0, T1)[t % 2][:, :].rearrange("p (k t) -> p k t", k=KT),
                   xh[:, :, t * P:(t + 1) * P]).then_inc(s_xl, 1)

            for b in range(B):
                dve.wait_ge(s_x[b], 16)
                ts = range(CH * b, CH * (b + 1))
                for t in ts:
                    st = dve.bn_stats(stats[:, t, :], y[:, t, :])
                st.then_inc(s_mv, 1)
                dve.wait_ge(s_mv, 3 * b + 1)
                for t in ts:
                    st = dve.bn_aggr(mv[:, t, :], stats[:, t, :])
                st.then_inc(s_mv, 1)
                dve.wait_ge(s_mv, 3 * b + 2)
                dve.tensor_scalar(sd[:, CH * b:CH * (b + 1)], mv[:, CH * b:CH * (b + 1), 1], EPS, None, ALU.add
                                  ).then_inc(s_ln, 1)
                dve.wait_ge(s_sd, b + 1)
                dve.reciprocal(sd[:, CH * b:CH * (b + 1)], sd[:, CH * b:CH * (b + 1)]).then_inc(s_mv, 1)
                dve.wait_ge(s_mv, 3 * b + 3)
                for t in ts:
                    if t >= 2:
                        dve.wait_ge(s_xtr, t - 1)
                    dve.tensor_scalar(o[:, 2 * (t % 2):2 * (t % 2) + 2, :].rearrange("p a d -> p (a d)"),
                                      y[:, t, :], mv[:, t, 0:1], sd[:, t:t + 1],
                                      ALU.subtract, ALU.mult).then_inc(s_xn, 1)
                    if t >= 1:
                        x_lo(t - 1)
            x_lo(TILES - 1)
            for k in range(2):
                lo_vg(0, k)
            clip(0, 0)
            for c in range(CH):
                gate(c, 0, 0)
            sums(0, 0)
            dve.wait_ge(s_const, 4)
            unit(0, 0)
            with dve.Fori(0, PAIRS - 1) as h:
                h_of[0] = h
                for i in range(1, B + 1):
                    unit(h * B + i, i)
            for i in range(1, B):
                unit((PAIRS - 1) * B + i, i, last=(i == B - 1), tail=True)
            norm_gate(UNITS - 1, B - 1)
            out_lo(UNITS - 1)
            for c in range(CH):
                add_y(UNITS - 1, B - 1, c)


def feed_forward(nc, sb_top, sem, fp8_scratch, gate_s, up_s, down_s, out, y, ident, bank):
    Y = bank[4:8]
    with ExitStack() as ctx:
        def sb(name, shape, dt=F32):
            return sb_top(name, shape, dt, ctx)

        xh, xl = (sb(n, [P, KT, B * T], F32R) for n in ("nT_hi", "nT_lo"))
        wg, wu = (sb(n, [P, KT, F], F32R) for n in ("w_gate", "w_up"))
        wd = sb("w_down", [P, FT, D], F32R)
        xn = sb("xn", [P, 2, D])
        gs, us = sb("gate_scale", [P, FT]), sb("up_scale", [P, FT])
        hgs, gus = sb("half_gate_scale", [P, FT]), sb("half_gate_up_scale", [P, FT])
        ds_row = sb("down_scale", [P, D])
        th, ga = (sb(n, [P, 2, T]) for n in ("tanh_half", "gated"))
        fh, fl = (sb(n, [P, 2, T], F32R) for n in ("fuse_hi", "fuse_lo"))
        res = sb("result", [P, CH, D])
        stats = sb("stats2", [P, TILES, 6])
        mv = sb("mean_var2", [P, TILES, 2])
        sd = sb("ln_rstd2", [P, TILES])

        s_w = sem("ffn_weights_loaded")
        s_sc = sem("ffn_scales_loaded")
        s_hgs, s_gus = sem("half_scale_ready"), sem("scale_product_ready")
        s_mv, s_var, s_sd = sem("n_stats_step"), sem("n_var_ready"), sem("n_sd_ready")
        s_xn, s_xtr, s_xh, s_xl = sem("n_ready"), sem("n_transposed"), sem("nT_hi_ready"), sem("nT_lo_ready")
        s_gu, s_th, s_ga, s_fu = sem("gate_up_done"), sem("tanh2_ready"), sem("gated_ready"), sem("fuse_ready")
        s_fh, s_fl, s_dn = sem("fuse_hi_ready"), sem("fuse_lo_ready"), sem("down_done")
        s_ys, s_res, s_out = sem("y_scaled"), sem("result_ready"), sem("result_stored")

        block = ctx.enter_context(nc.Block())

        @block.sync
        def _(sp):
            for n, (w, a) in enumerate(((wg, KT), (wu, KT), (wd, FT))):
                src = fp8_scratch[n].rearrange("p c -> (p c)").rearrange("(k q n) -> q k n", k=a, q=P)
                sp.dma_start(w[:, :, :].bitcast(F32), src).then_inc(s_w, 16)
            with nc.allow_non_contiguous_dma(reason="per-feature scales, once"):
                sp.dma_start(gs[:, :], gate_s.rearrange("(f p) -> p f", p=P)).then_inc(s_sc, 16)
                sp.dma_start(us[:, :], up_s.rearrange("(f p) -> p f", p=P)).then_inc(s_sc, 16)
            sp.dma_start(ds_row[:, :], down_s.rearrange("(a n) -> a n", a=1).broadcast_to([P, D])
                         ).then_inc(s_sc, 16)
            with sp.Fori(0, B) as b:
                for c in range(CH):
                    sp.wait_ge(s_res, b * CH + c + 1)
                    sp.dma_start(out[b, P * c:P * (c + 1), :] if isinstance(b, int) else
                                 out.rearrange("b (c p) d -> (b c) p d", p=P)[bass.ds(b * CH + c, 1), :, :]
                                 .rearrange("a p d -> (a p) d"), res[:, c, :]).then_inc(s_out, 16)
            sp.wait_ge(s_out, 16 * TILES)

        @block.tensor
        def _(pe):
            for t in range(TILES):
                pe.wait_ge(s_xn, t + 1)
                if t >= 2:
                    pe.wait_ge(s_xl, t - 1)
                for k in range(KT):
                    mm = pe.transpose(bank[t % 2][:, k * P:(k + 1) * P], xn[:, t % 2, k * P:(k + 1) * P],
                                      ident[:, :])
                mm.then_inc(s_xtr, 1)
            pe.wait_ge(s_xl, TILES)
            pe.wait_ge(s_w, 48)

            def gate_up(b, f, n):
                if not (isinstance(b, int) and n < 2):
                    pe.wait_ge(s_fu, b * FT + f - 1)
                for w, dst in ((wg, bank[2 * (f % 2)]), (wu, bank[2 * (f % 2) + 1])):
                    for k in range(KT):
                        for part in (xh, xl):
                            mm = pe.matmul(dst[:, :], w[:, k, f * P:(f + 1) * P], part[:, k, bass.ds(b * T, T)],
                                           start=(k == 0 and part is xh), stop=(k == KT - 1 and part is xl))
                mm.then_inc(s_gu, 1)

            def tokens(b, first):
                for f in range(FT):
                    if f + 1 < FT:
                        gate_up(b, f + 1, f + 1 if first else FT)
                    pe.wait_ge(s_fh, b * FT + f + 1)
                    pe.wait_ge(s_fl, b * FT + f + 1)
                    if f == 0 and not first:
                        pe.wait_ge(s_ys, b * CH)
                    for c in range(CH):
                        for part in (fh, fl):
                            mm = pe.matmul(Y[c][:, :], part[:, f % 2, c * P:(c + 1) * P], wd[:, f, :],
                                           start=(f == 0 and part is fh), stop=(f == FT - 1 and part is fl))
                    mm.then_inc(s_dn, 1)

            gate_up(0, 0, 0)
            tokens(0, True)
            with pe.Fori(1, B) as b:
                gate_up(b, 0, FT)
                tokens(b, False)

        @block.scalar
        def _(act):
            act.wait_ge(s_sc, 48)
            act.mul(hgs[:, :], gs[:, :], 0.5).then_inc(s_hgs, 1)
            for t in range(-1, TILES):
                if t % CH == CH - 1 and t < TILES - 1:
                    b = (t + 1) // CH
                    act.wait_ge(s_var, b + 1)
                    act.activation(sd[:, CH * b:CH * (b + 1)], sd[:, CH * b:CH * (b + 1)], ACT.Sqrt
                                   ).then_inc(s_sd, 1)
                if t < 0:
                    continue
                act.wait_ge(s_xtr, t + 1)
                act.activation(xh[:, :, t * P:(t + 1) * P], bank[t % 2][:, :].rearrange("p (k t) -> p k t", k=KT),
                               ACT.Copy).then_inc(s_xh, 1)
            act.wait_ge(s_hgs, 1)

            def feature(b, f, early):
                act.wait_ge(s_gu, b * FT + f + 1)
                if not early:
                    act.wait_ge(s_ga, b * FT + f - 1)
                act.activation(th[:, f % 2, :], bank[2 * (f % 2)][:, :], ACT.Tanh, scale=hgs[:, f:f + 1]
                               ).then_inc(s_th, 1)

            def fuse_hi(b, f, early):
                act.wait_ge(s_fu, b * FT + f + 1)
                if not early:
                    act.wait_ge(s_dn, b * FT + f - 1)
                act.activation(fh[:, f % 2, :], ga[:, f % 2, :], ACT.Copy).then_inc(s_fh, 1)

            for f in range(FT):
                feature(0, f, f < 2)
                fuse_hi(0, f, f < 2)
            with act.Fori(1, B) as b:
                for f in range(FT):
                    feature(b, f, False)
                    fuse_hi(b, f, False)

        @block.vector
        def _(dve):
            for b in range(B):
                ts = range(CH * b, CH * (b + 1))
                for t in ts:
                    st = dve.bn_stats(stats[:, t, :], y[:, t, :])
                st.then_inc(s_mv, 1)
                dve.wait_ge(s_mv, 3 * b + 1)
                for t in ts:
                    st = dve.bn_aggr(mv[:, t, :], stats[:, t, :])
                st.then_inc(s_mv, 1)
                dve.wait_ge(s_mv, 3 * b + 2)
                dve.tensor_scalar(sd[:, CH * b:CH * (b + 1)], mv[:, CH * b:CH * (b + 1), 1], EPS, None, ALU.add
                                  ).then_inc(s_var, 1)
                dve.wait_ge(s_sd, b + 1)
                dve.reciprocal(sd[:, CH * b:CH * (b + 1)], sd[:, CH * b:CH * (b + 1)]).then_inc(s_mv, 1)
                dve.wait_ge(s_mv, 3 * b + 3)
                for t in ts:
                    if t >= 2:
                        dve.wait_ge(s_xtr, t - 1)
                    dve.tensor_scalar(xn[:, t % 2, :], y[:, t, :], mv[:, t, 0:1], sd[:, t:t + 1],
                                      ALU.subtract, ALU.mult).then_inc(s_xn, 1)
                    for last in ((t - 1,) if 1 <= t < TILES - 1 else (t - 1, t) if t else ()):
                        dve.wait_ge(s_xh, last + 1)
                        dve.tensor_tensor(xl[:, :, last * P:(last + 1) * P],
                                          bank[last % 2][:, :].rearrange("p (k t) -> p k t", k=KT),
                                          xh[:, :, last * P:(last + 1) * P].bitcast(F32), ALU.subtract
                                          ).then_inc(s_xl, 1)
            dve.wait_ge(s_hgs, 1)
            dve.tensor_tensor(gus[:, :], hgs[:, :], us[:, :], ALU.mult).then_inc(s_gus, 1)
            dve.wait_ge(s_gus, 1)

            def tokens(b, first):
                for f in range(FT):
                    dve.wait_ge(s_th, b * FT + f + 1)
                    if not (first and f < 2):
                        dve.wait_ge(s_fl, b * FT + f - 1)
                        dve.wait_ge(s_fh, b * FT + f - 1)
                    dve.scalar_tensor_tensor(out=ga[:, f % 2, :], in0=th[:, f % 2, :], scalar=1.0,
                                             in1=bank[2 * (f % 2)][:, :], op0=ALU.add, op1=ALU.mult
                                             ).then_inc(s_ga, 1)
                    dve.wait_ge(s_ga, b * FT + f + 1)
                    dve.scalar_tensor_tensor(out=ga[:, f % 2, :], in0=ga[:, f % 2, :], scalar=gus[:, f:f + 1],
                                             in1=bank[2 * (f % 2) + 1][:, :], op0=ALU.mult, op1=ALU.mult
                                             ).then_inc(s_fu, 1)
                    dve.wait_ge(s_fh, b * FT + f + 1)
                    dve.tensor_tensor(fl[:, f % 2, :], ga[:, f % 2, :], fh[:, f % 2, :].bitcast(F32),
                                      ALU.subtract).then_inc(s_fl, 1)
                dve.wait_ge(s_dn, b * FT + FT)
                for c in range(CH):
                    if not first:
                        dve.wait_ge(s_out, b * 16 * CH)
                    dve.tensor_tensor(res[:, c, :], Y[c][:, :], ds_row[:, :], ALU.mult).then_inc(s_ys, 1)
                for c in range(CH):
                    dve.wait_ge(s_ys, b * CH + c + 1)
                    dve.tensor_tensor(res[:, c, :], res[:, c, :],
                                      y[:, c, :] if first else y[:, bass.ds(b * CH + c, 1), :].rearrange(
                                          "p a d -> p (a d)"), ALU.add).then_inc(s_res, 1)

            tokens(0, True)
            with dve.Fori(1, B) as b:
                tokens(b, False)


_INS = ["L0_attn_hidden_states", "L0_attn_Wq", "L0_attn_Wk", "L0_attn_Wv", "L0_attn_Wg", "L0_attn_Ws",
        "L0_attn_Wo", "L0_attn_g_norm_weight", "L0_ffn_gate_w", "L0_ffn_up_w", "L0_ffn_down_w",
        "L0_ffn_gate_scale", "L0_ffn_up_scale", "L0_ffn_down_scale"]


def kernel(**inputs):
    import numpy as _np
    import concourse.bacc as _bacc
    from concourse import mybir as _mybir
    from concourse.bass_utils import run_bass_kernel_spmd as _run

    nc = _bacc.Bacc("TRN2", target_bir_lowering=False, num_devices=1)
    arrays, args = {}, []
    for name in _INS:
        a = _np.ascontiguousarray(inputs[name])
        arrays[f"in_{name}"] = a
        args.append(nc.dram_tensor(f"in_{name}", a.shape, _mybir.dt.from_np(a.dtype), kind="ExternalInput").ap())
    args.append(nc.dram_tensor("out_0", (B, T, D), F32, kind="ExternalOutput").ap())
    gsa_swiglu(nc, *args)
    r = _run(nc, [arrays], core_ids=[0])
    return r.results[0]["out_0"]
```

```python
from contextlib import ExitStack

import concourse.bass as bass
from concourse import mybir
from concourse.alu_op_type import AluOpType as ALU

F32 = mybir.dt.float32
F32R = mybir.dt.float32r
I32 = mybir.dt.int32
ACT = mybir.ActivationFunctionType
AX = mybir.AxisListType

P = 128
B, T, D = 4, 512, 512
H, DK, DV, M = 16, 64, 128, 64
F = 1536
KT = D // P
CH = T // P
PAIRS = H // 2
UNITS = PAIRS * B
TILES = B * CH
FT = F // P
EPS = 1e-5
CLAMP = 32.0
SCALE = DK ** -0.5
FP8_MAX = 448.0
FP8_MIN_NORMAL = 2.0 ** -6
ROUNDER = 1.5 * 2.0 ** 20
HUGE = 3.0e38
Q8_STEPS = 8
QF = D * F // P
QC = 212
QC0 = QF - QC * (UNITS - B)
assert 0 < QC0 <= QC
EARLY = 4

ST, VG0, QT, VG1, KTJ, VG2, VG3 = range(7)
JOBS = 7


def gsa_swiglu(nc, x, Wq, Wk, Wv, Wg, Ws, Wo, gnorm, gate_w, up_w, down_w, gate_s, up_s, down_s, out):
    fp8_scratch = nc.dram_tensor("fp8_weights", (3, P, QF), F32, kind="Internal").ap()
    flat = [w.rearrange("a b -> (a b)").rearrange("(p c) -> p c", p=P) for w in (gate_w, up_w, down_w)]

    top = ExitStack()
    with top:
        def sb(name, shape, dt=F32, ctx=top):
            return ctx.enter_context(nc.sbuf_tensor(name, shape, dt))

        def sem(name):
            return top.enter_context(nc.semaphore(name))

        y = sb("y", [P, TILES, D])
        ident = sb("ident", [P, P])
        bank = [top.enter_context(nc.psum_tensor(f"bank{i}", [P, 512], F32)) for i in range(8)]

        xh, xl = (sb(n, [P, KT, B * T], F32R) for n in ("xT_hi", "xT_lo"))
        vgh, vgl = (sb(n, [P, KT, 2 * 2 * DV], F32R) for n in ("wvg_hi", "wvg_lo"))
        neg_half = sb("neg_half", [P, 2 * CH])

        s_early = sem("early_gate_up_loaded")
        shared = (y, ident, bank, xh, xl, vgh, vgl, neg_half, s_early)
        attention(nc, sb, sem, x, Wq, Wk, Wv, Wg, Ws, Wo, gnorm, flat, fp8_scratch, shared)
        feed_forward(nc, sb, sem, fp8_scratch, gate_s, up_s, down_s, out, shared)


def gate_up_columns(scratch, k_tiles, f0, f1):
    return scratch.rearrange("p c -> (p c)").rearrange("(k q n) -> q k n", k=k_tiles, q=P)[:, :, f0 * P:f1 * P]


def norm_stats(dve, y, b, stats, mv, sd, s_step, s_var):
    for c in range(CH):
        st = dve.bn_stats(stats[:, c, :], y[:, CH * b + c, :])
    st.then_inc(s_step[0], 1)
    dve.wait_ge(s_step[0], s_step[1] + 1)
    for c in range(CH):
        st = dve.bn_aggr(mv[:, c, :], stats[:, c, :])
    st.then_inc(s_step[0], 1)
    dve.wait_ge(s_step[0], s_step[1] + 2)
    dve.tensor_scalar(sd, mv[:, :, 1], EPS, None, ALU.add).then_inc(s_var, 1)


def attention(nc, sb_top, sem, x, Wq, Wk, Wv, Wg, Ws, Wo, gnorm, flat, fp8_scratch, shared):
    y, ident, bank, xh, xl, vgh, vgl, neg_half, s_early = shared
    PJ, A, (T0, T1, T2, T3) = bank[0:2], bank[2:4], bank[4:8]

    with ExitStack() as ctx:
        def sb(name, shape, dt=F32):
            return sb_top(name, shape, dt, ctx)

        wh = {n: sb(f"w{n}_hi", [P, KT, P], F32R) for n in "sqk"}
        wl = {n: sb(f"w{n}_lo", [P, KT, P], F32R) for n in "sqk"}
        woh, wol = (sb(n, [P, 2, D], F32R) for n in ("wo_hi", "wo_lo"))
        stage = sb("stage", [P, D])
        stage_vg = sb("stage_vg", [P, KT, 4 * DV])

        qT, kT = sb("qT", [P, T]), sb("kT", [P, T])
        k_tok, e_tok, c_inv = (sb(n, [P, CH, P]) for n in ("k_tok", "e_tok", "c_inv"))
        eT = [sb(f"eT{i}", [P, T]) for i in range(2)]
        cT = [sb(f"cT{i}", [P, T]) for i in range(2)]
        v = [sb(f"v{i}", [P, CH, 2 * DV]) for i in range(2)]
        g = [sb(f"g{i}", [P, CH, 2 * DV]) for i in range(2)]
        th = sb("tanh_half_g", [P, 2 * DV])
        aT = sb("aT", [P, 2, CH, P])
        hk = sb("hk", [P, CH - 1, P])
        hv = sb("hv", [P, CH - 1, 2 * DV])
        p = sb("p", [P, CH * P])
        wT = sb("wT", [P, T])
        o = sb("o", [P, CH, 2 * DV])
        oh, ol = (sb(n, [P, 2, T], F32R) for n in ("oT_hi", "oT_lo"))
        q8 = sb("q8", [P, 3, QC])
        q8t = sb("q8t", [P, 3, QC])
        tri = sb("tri", [P, P])
        half_gn = sb("half_gn", [P, 1])
        ssq, rstd = sb("ssq", [P, 2 * CH]), sb("rstd", [P, 2 * CH])
        mx, sm, rs = (sb(n, [P, 2 * CH]) for n in ("slot_max", "slot_sum", "slot_rsum"))
        q8_flat, q8t_flat = (q[:, :, :].rearrange("p a b -> p (a b)") for q in (q8, q8t))
        xn2 = [q[:, 0:D] for q in (q8_flat, q8t_flat)]
        stats = [q8_flat[:, D + 24 * b:D + 24 * (b + 1)].rearrange("p (t s) -> p t s", s=6) for b in range(B)]
        mv = [q8t_flat[:, D + 8 * b:D + 8 * (b + 1)].rearrange("p (t s) -> p t s", s=2) for b in range(B)]
        sd = [q8t_flat[:, D + 32 + CH * b:D + 32 + CH * (b + 1)] for b in range(B)]

        s_const = sem("const_ready")
        s_x = [sem(f"x_loaded{b}") for b in range(B)]
        s_fp8_out = sem("fp8_stored")
        s_gn = sem("gnorm_loaded")
        s_mv, s_var = sem("ln_stats_step"), sem("ln_var_ready")
        s_n, s_ntr = sem("n_ready"), sem("n_transposed")
        s_nh, s_nl = sem("nT_hi_ready"), sem("nT_lo_ready")
        s_sd = sem("ln_sd_ready")
        s_neg = sem("exponent_ready")
        s_zero, s_gnh = sem("states_zeroed"), sem("half_gnorm_ready")
        s_xn = sem("ln_x_ready")
        s_xtr = sem("ln_x_transposed")
        s_xh, s_xl = sem("xT_hi_ready"), sem("xT_lo_ready")
        s_stage, s_stage_vg = sem("stage_loaded"), [sem(f"stage_vg_loaded{k}") for k in range(KT)]
        s_wh, s_wl = sem("w_hi_ready"), sem("w_lo_ready")
        s_vgh = sem("vg_hi_ready")
        s_vgl, s_vgl2 = sem("vg_lo_ready"), sem("vg_lo_2_ready")
        s_wos = sem("wo_scaled")
        s_job = sem("job_done")
        s_clip, s_q, s_k, s_e = sem("s_clipped"), sem("q_ready"), sem("k_ready"), sem("e_ready")
        s_scan, s_cinv = sem("c_summed"), sem("c_inverted")
        s_v, s_th, s_g = sem("v_ready"), sem("tanh_ready"), sem("g_ready")
        s_trk, s_tre, s_trc = sem("k_transposed"), sem("e_transposed"), sem("c_transposed")
        s_ktok, s_etok, s_ctok = sem("k_tok_ready"), sem("e_tok_ready"), sem("c_inv_ready")
        s_a, s_am = sem("scores_done"), sem("scores_masked")
        s_hkd, s_hk = sem("hk_parts_done"), sem("hk_step")
        s_hvd, s_hv = sem("hv_parts_done"), sem("hv_step")
        s_ok, s_okn = sem("ok_done"), sem("softmax_step")
        s_exp = sem("slot_exp_ready")
        s_trw, s_wT = sem("w_transposed"), sem("wT_ready")
        s_b, s_bm = sem("value_weights_done"), sem("value_weights_masked")
        s_o, s_ocp, s_sq = sem("o_done"), sem("o_copied"), sem("o_squared")
        s_ms, s_rstd, s_og = sem("o_mean_square"), sem("o_rstd_ready"), sem("o_gated")
        s_tro, s_oh, s_ol = sem("o_transposed"), sem("oT_hi_ready"), sem("oT_lo_ready")
        s_y, s_ya = sem("y_done"), sem("y_added")
        s_q8in, s_q8 = sem("fp8_in_loaded"), sem("fp8_step")

        block = ctx.enter_context(nc.Block())

        def tokens_after(j):
            return range(CH + 2 * (j - 1), CH + 2 * j) if j else ()

        def split_next(i, tail):
            return i == 2 and not tail, i in (0, B)

        @block.sync
        def _(sp):
            def load_x(b):
                sp.dma_start(y[:, CH * b:CH * (b + 1), :],
                             x[b].rearrange("(c p) d -> p c d", p=P)).then_inc(s_x[b], 16)

            load_x(0)
            sp.dma_start(half_gn[:, :], gnorm.rearrange("(p a) -> p a", a=1)).then_inc(s_gn, 16)

            def load_sqk(pair, n):
                if not (isinstance(pair, int) and n == 0):
                    sp.wait_ge(s_wl, pair * 5 + n)
                sp.dma_start(stage[:, :].rearrange("p (k n) -> p k n", k=KT),
                             (Ws, Wq, Wk)[n].rearrange("(k p) n -> p k n", p=P)[:, :, bass.ds(pair * P, P)]
                             ).then_inc(s_stage, 16)

            def load_vg(pair):
                for k in range(KT):
                    if not isinstance(pair, int):
                        sp.wait_ge((s_vgl, s_vgl2)[k // 2], (pair - 1) * 2 + k % 2 + 1)
                    for n, w in enumerate((Wv, Wg)):
                        sp.dma_start(stage_vg[:, k, n * 2 * DV:(n + 1) * 2 * DV],
                                     w[P * k:P * (k + 1), bass.ds(pair * 2 * DV, 2 * DV)]
                                     ).then_inc(s_stage_vg[k], 16)

            def load_o(pair, a):
                sp.wait_ge(s_wl, pair * 5 + 3 + a)
                sp.dma_start(stage[:, :], Wo[bass.ds(pair * 2 * DV + a * DV, DV), :]).then_inc(s_stage, 16)

            def slice_of(u):
                return (0, QC0) if isinstance(u, int) else ((u - 1) * QC + QC0, QC)

            def load_q8(u):
                if isinstance(u, int):
                    sp.wait_ge(s_xn, TILES)
                else:
                    sp.wait_ge(s_fp8_out, 16 * u)
                start, n = slice_of(u)
                for m, w in enumerate(flat):
                    sp.dma_start(q8[:, m, 0:n], w[:, bass.ds(start, n)]).then_inc(s_q8in, 16)

            def store_q8(u):
                sp.wait_ge(s_q8, Q8_STEPS * (u + 1))
                start, n = slice_of(u)
                sp.dma_start(fp8_scratch[:, :, bass.ds(start, n)].rearrange("n p c -> p n c"),
                             q8[:, :, 0:n]).then_inc(s_fp8_out, 16)

            load_sqk(0, 0)
            load_vg(0)
            load_x(1)
            load_sqk(0, 1)
            load_x(2)
            load_sqk(0, 2)
            load_x(3)
            load_o(0, 0)
            load_q8(0)
            load_o(0, 1)
            store_q8(0)
            with sp.Fori(0, PAIRS - 1) as h:
                for i in range(1, B + 1):
                    load_q8(h * B + i)
                    if i == 1:
                        load_sqk(h + 1, 0)
                        load_vg(h + 1)
                    if i == 2:
                        load_sqk(h + 1, 1)
                        load_sqk(h + 1, 2)
                        load_o(h + 1, 0)
                    if i == B:
                        load_o(h + 1, 1)
                    store_q8(h * B + i)
            sp.wait_ge(s_fp8_out, 16 * (UNITS - B + 1))
            sp.wait_ge(s_job, JOBS * UNITS)
            for n, w in enumerate((vgh, vgl)):
                sp.dma_start(w[:, :, :].bitcast(F32), gate_up_columns(fp8_scratch[n], KT, 0, EARLY)
                             ).then_inc(s_early, 16)

        @block.tensor
        def _(pe):
            def product3(dst, pairs):
                n = len(pairs)
                for k, (w_hi, w_lo, m_hi, m_lo) in enumerate(pairs):
                    pe.matmul(dst, w_hi, m_hi, start=(k == 0), stop=False)
                    pe.matmul(dst, w_hi, m_lo, start=False, stop=False)
                    last = pe.matmul(dst, w_lo, m_hi, start=False, stop=(k == n - 1))
                return last

            def job(j, u, i):
                b = i % B
                dst = PJ[(JOBS * i + j) % 2]
                first = isinstance(u, int) and u == 0
                if j == ST:
                    if not first:
                        pe.wait_ge(s_v, u * CH - 1)
                        pe.wait_ge(s_g, u * CH - 1)
                    if b == 0:
                        pe.wait_ge(s_wl, 5 * pair_of(u, i) + 1)
                    if not isinstance(u, int) or u < B:
                        pe.wait_ge(s_xl, CH * (b + 1))
                elif j == VG0:
                    if not first:
                        pe.wait_ge(s_v, u * CH)
                        pe.wait_ge(s_g, u * CH)
                    if b == 0:
                        pe.wait_ge(s_vgl, 2 * pair_of(u, i) + 2)
                        pe.wait_ge(s_vgl2, 2 * pair_of(u, i) + 2)
                elif j == QT:
                    pe.wait_ge(s_clip, u + 1)
                    if b == 0:
                        pe.wait_ge(s_wl, 5 * pair_of(u, i) + 2)
                elif j == VG1:
                    pe.wait_ge(s_v, u * CH + 1)
                    pe.wait_ge(s_g, u * CH + 1)
                elif j == KTJ:
                    pe.wait_ge(s_q, u + 1)
                    if b == 0:
                        pe.wait_ge(s_wl, 5 * pair_of(u, i) + 3)
                elif j == VG2:
                    pe.wait_ge(s_v, u * CH + 2)
                    pe.wait_ge(s_g, u * CH + 2)
                elif j == VG3:
                    pe.wait_ge(s_k, u + 1)
                if j in (ST, QT, KTJ):
                    n = {ST: "s", QT: "q", KTJ: "k"}[j]
                    cols = slice(T * b, T * (b + 1))
                    last = product3(dst[:, :], [(wh[n][:, k, :], wl[n][:, k, :], xh[:, k, cols], xl[:, k, cols])
                                                for k in range(KT)])
                else:
                    c = {VG0: 0, VG1: 1, VG2: 2, VG3: 3}[j]
                    cols = slice(T * b + P * c, T * b + P * (c + 1))
                    last = product3(dst[:, :], [(xh[:, k, cols], xl[:, k, cols], vgh[:, k, :], vgl[:, k, :])
                                                for k in range(KT)])
                last.then_inc(s_job, 1)

            def pair_of(u, i):
                return u // B if isinstance(u, int) else pair_reg[0] + i // B

            pair_reg = [None]

            def out_transposes(u):
                pe.wait_ge(s_og, u + 1)
                pe.wait_ge(s_am, 2 * (u + 1) + 2) if not last_tail[0] else pe.wait_ge(s_bm, 2 * (u + 1))
                for a in range(2):
                    for c in range(CH):
                        last = pe.transpose(A[a][:, c * P:(c + 1) * P], o[:, c, a * DV:(a + 1) * DV], ident[:, :])
                    last.then_inc(s_tro, 1)

            def out_product(u, pair_ready):
                pe.wait_ge(s_oh, 2 * (u + 1))
                pe.wait_ge(s_ol, 2 * (u + 1))
                if pair_ready is not None:
                    pe.wait_ge(s_wl, pair_ready)
                for c, dst in enumerate((T2, A[0], A[1], T0)):
                    if c == 3:
                        pe.wait_ge(s_okn, 6 * (u + 1) + 1 if not last_tail[0] else 6 * (u + 1))
                    cols = slice(c * P, (c + 1) * P)
                    product3(dst[:, :], [(oh[:, a, cols], ol[:, a, cols], woh[:, a, :], wol[:, a, :])
                                         for a in range(2)]).then_inc(s_y, 1)

            last_tail = [False]

            def unit(u, i, last=False, tail=False):
                par = i % 2
                first = isinstance(u, int) and u == 0
                nu, ni = u + 1, i + 1
                pe.wait_ge(s_k, u + 1)
                if not first:
                    pe.wait_ge(s_okn, 6 * (u - 1) + 1)
                for c in range(CH):
                    mm = pe.transpose(T0[:, c * P:(c + 1) * P], kT[:, c * P:(c + 1) * P], ident[:, :])
                mm.then_inc(s_trk, 1)
                pe.wait_ge(s_q, u + 1)
                if not first:
                    pe.wait_ge(s_bm, 2 * u)
                for c in range(CH):
                    for a in range(2):
                        hs, cs = slice(DK * a, DK * (a + 1)), slice(c * P, (c + 1) * P)
                        mm = pe.matmul(A[a][:, cs], kT[hs, cs], qT[hs, cs], start=True, stop=True)
                mm.then_inc(s_a, 1)
                pe.wait_ge(s_e, u + 1)
                if not first:
                    pe.wait_ge(s_sq, 2 * CH * u)
                for c in range(CH):
                    mm = pe.transpose(T1[:, c * P:(c + 1) * P], eT[par][:, c * P:(c + 1) * P], ident[:, :])
                mm.then_inc(s_tre, 1)
                pe.wait_ge(s_cinv, u + 1)
                if not first:
                    pe.wait_ge(s_wT, u)
                for c in range(CH):
                    mm = pe.transpose(T2[:, c * P:(c + 1) * P], cT[par][:, c * P:(c + 1) * P], ident[:, :])
                mm.then_inc(s_trc, 1)
                if not last:
                    job(ST, nu, ni)
                if tail and i >= 2:
                    norm_transposes(i - 2, (0, 1), (T1, T2))
                pe.wait_ge(s_ktok, u + 1)
                pe.wait_ge(s_etok, u + 1)
                for c in range(CH - 1):
                    mm = pe.matmul(T3[:, c * P:(c + 1) * P], k_tok[:, c, :], e_tok[:, c, :], start=True, stop=True)
                mm.then_inc(s_hkd, 1)
                if not last:
                    job(VG0, nu, ni)
                if tail and i >= 2:
                    pe.wait_ge(s_nl, CH * (i - 2) + 2)
                    norm_transposes(i - 2, (2, 3), (T1, T2))
                pe.wait_ge(s_am, 2 * u + 2)
                pe.wait_ge(s_hk, 3 * (u + 1))
                for c in range(CH):
                    if c:
                        pe.matmul(T0[:, c * P:(c + 1) * P], qT[:, c * P:(c + 1) * P], hk[:, c - 1, :],
                                  start=False, stop=False, skip_group_check=True)
                    for a in range(2):
                        mm = pe.matmul(T0[:, c * P + a * M:c * P + (a + 1) * M], aT[:, a, c, :],
                                       e_tok[:, c, a * M:(a + 1) * M], start=(c == 0 and a == 0),
                                       stop=(c == CH - 1 and a == 1), skip_group_check=True)
                mm.then_inc(s_ok, 1)
                pe.wait_ge(s_v, (u + 1) * CH)
                if tail and i >= 2:
                    pe.wait_ge(s_nl, CH * (i - 1))
                for c in range(CH - 1):
                    dst = (T1[:, 0:256], T1[:, 256:512], T3[:, 0:256])[c]
                    mm = pe.matmul(dst, e_tok[:, c, :], v[par][:, c, :], start=True, stop=True)
                mm.then_inc(s_hvd, 1)
                if not first:
                    out_transposes(u - 1)
                if not last:
                    job(QT, nu, ni)
                if not first:
                    pe.wait_ge(s_ctok, u + 1)
                    out_product(u - 1, wo_ready(u, i))
                pe.wait_ge(s_okn, 6 * (u + 1))
                if not first:
                    pe.wait_ge(s_ya, u * CH - 3)
                for c in range(CH):
                    mm = pe.transpose(T2[:, c * P:(c + 1) * P], p[:, c * P:(c + 1) * P], ident[:, :])
                mm.then_inc(s_trw, 1)
                if not last:
                    job(VG1, nu, ni)
                    job(KTJ, nu, ni)
                pe.wait_ge(s_wT, u + 1)
                if not first:
                    pe.wait_ge(s_ya, u * CH)
                for c in range(CH):
                    for a in range(2):
                        hs, cs = slice(M * a, M * (a + 1)), slice(c * P, (c + 1) * P)
                        mm = pe.matmul(A[a][:, cs], eT[par][hs, cs], wT[hs, cs], start=True, stop=True)
                mm.then_inc(s_b, 1)
                if not last:
                    job(VG2, nu, ni)
                pe.wait_ge(s_bm, 2 * (u + 1))
                pe.wait_ge(s_hv, 3 * (u + 1))
                for c in range(CH):
                    bk, at = (T1, T3)[c // 2], (c % 2) * 2 * DV
                    if c:
                        mm = pe.matmul(bk[:, at:at + 2 * DV], wT[:, c * P:(c + 1) * P], hv[:, c - 1, :],
                                       start=(c == 2), stop=False, skip_group_check=True)
                    for a in range(2):
                        mm = pe.matmul(bk[:, at + a * DV:at + (a + 1) * DV], aT[:, a, c, :],
                                       v[par][:, c, a * DV:(a + 1) * DV], start=(c == 0 and a == 0),
                                       stop=(a == 1 and c % 2 == 1), skip_group_check=True)
                    if c % 2:
                        mm.then_inc(s_o, 1)
                if not last:
                    job(VG3, nu, ni)

            def wo_ready(u, i):
                if i % B != 1:
                    return None
                return 5 * (u // B if isinstance(u, int) else pair_reg[0]) + 5

            def norm_transposes(b, tiles, banks):
                for c, dst in zip(tiles, banks):
                    t = CH * b + c
                    pe.wait_ge(s_n, t + 1)
                    if c < 2 and b < 2:
                        pe.wait_ge((s_etok, s_ctok)[c], UNITS - 1 + b)
                    for k in range(KT):
                        mm = pe.transpose(dst[:, k * P:(k + 1) * P], xn2[t % 2][:, k * P:(k + 1) * P], ident[:, :])
                    mm.then_inc(s_ntr, 1)

            def token_transposes(t):
                pe.wait_ge(s_xn, t + 1)
                if t >= 2:
                    pe.wait_ge(s_xl, t - 1)
                for k in range(KT):
                    mm = pe.transpose((T0, T1)[t % 2][:, k * P:(k + 1) * P],
                                      o[:, 2 * (t % 2):2 * (t % 2) + 2, :].rearrange("p a d -> p (a d)")
                                      [:, k * P:(k + 1) * P], ident[:, :])
                mm.then_inc(s_xtr, 1)

            pe.wait_ge(s_const, 4)
            for t in range(CH):
                token_transposes(t)
            for j in range(JOBS):
                job(j, 0, 0)
                for t in tokens_after(j):
                    token_transposes(t)
            pe.wait_ge(s_xl, TILES)
            unit(0, 0)
            with pe.Fori(0, PAIRS - 1) as h:
                pair_reg[0] = h
                for i in range(1, B + 1):
                    unit(h * B + i, i)
            for i in range(1, B):
                unit((PAIRS - 1) * B + i, i, last=(i == B - 1), tail=True)
            last_tail[0] = True
            pe.wait_ge(s_g, CH * UNITS)
            pe.wait_ge(s_v, CH * UNITS)
            norm_transposes(2, (0, 1), PJ)
            norm_transposes(2, (2, 3), (T0, T2))
            out_transposes(UNITS - 1)
            out_product(UNITS - 1, None)

        @block.scalar
        def _(act):
            def copy(dst, src):
                return act.activation(dst, src, ACT.Copy)

            def split_w(n, dst, count):
                act.wait_ge(s_stage, 16 * count)
                copy(dst, stage[:, :].rearrange("p (k n) -> p k n", k=KT)).then_inc(s_wh, 1)

            def split_next_w(n, j, nu):
                act.wait_ge(s_job, nu * JOBS + j + 1)
                split_w(n, wh["sqk"[n]][:, :, :], (h_of[0] + 1) * 5 + n + 1)

            def split_vg(pair, k):
                act.wait_ge(s_stage_vg[k], (pair + 1) * 32)
                copy(vgh[:, k, :], stage_vg[:, k, :]).then_inc(s_vgh, 1)

            def split_o(pair, a):
                act.wait_ge(s_stage, (pair * 5 + 4 + a) * 16)
                act.activation(stage[:, :], stage[:, :], ACT.Copy, scale=half_gn[:, 0:1]).then_inc(s_wos, 1)
                act.wait_ge(s_wos, pair * 2 + a + 1)
                copy(woh[:, a, :], stage[:, :]).then_inc(s_wh, 1)

            def evac(j, u, i):
                par = i % 2
                src = PJ[(JOBS * i + j) % 2]
                first = isinstance(u, int) and u == 0
                if j == ST:
                    act.wait_ge(s_clip, u + 1)
                    act.activation(eT[par][:, :], eT[par][:, :], ACT.Exp).then_inc(s_e, 1)
                    return
                act.wait_ge(s_job, u * JOBS + j + 1)
                if j == QT:
                    if not first:
                        act.wait_ge(s_ok, u)
                    copy(qT[:, :], src[:, :]).then_inc(s_q, 1)
                elif j == KTJ:
                    if not first:
                        act.wait_ge(s_a, u)
                    copy(kT[:, :], src[:, :]).then_inc(s_k, 1)
                else:
                    c = {VG0: 0, VG1: 1, VG2: 2, VG3: 3}[j]
                    if not isinstance(u, int) or u >= 2:
                        act.wait_ge(s_o, 2 * (u - 1))
                    copy(v[par][:, c, :], src[:, 0:2 * DV]).then_inc(s_v, 1)
                    if not (first and c == 0):
                        act.wait_ge(s_g, u * CH + c)
                    act.activation(th[:, :], src[:, 2 * DV:4 * DV], ACT.Tanh, scale=0.5).then_inc(s_th, 1)

            def norm_hi(b, tiles, banks):
                for c, src in zip(tiles, banks):
                    t = CH * b + c
                    act.wait_ge(s_ntr, t + 1)
                    copy(xh[:, :, t * P:(t + 1) * P], src[:, :].rearrange("p (k t) -> p k t", k=KT)
                         ).then_inc(s_nh, 1)

            def out_hi(u):
                for a in range(2):
                    act.wait_ge(s_tro, 2 * u + a + 1)
                    if a == 0 and not (isinstance(u, int) and u == 0):
                        act.wait_ge(s_y, CH * u)
                    copy(oh[:, a, :], A[a][:, :]).then_inc(s_oh, 1)

            def unit(u, i, last=False, tail=False):
                first = isinstance(u, int) and u == 0
                nu, ni = u + 1, i + 1
                act.wait_ge(s_trk, u + 1)
                if not first:
                    act.wait_ge(s_hkd, u)
                copy(k_tok[:, :, :].rearrange("p c m -> p (c m)"), T0[:, :]).then_inc(s_ktok, 1)
                if i == 3 and not tail:
                    act.wait_ge(s_job, u * JOBS + VG3 + 1)
                    for k in range(KT):
                        split_vg(h_of[0] + 1, k)
                act.wait_ge(s_tre, u + 1)
                if not first:
                    act.wait_ge(s_hvd, u)
                copy(e_tok[:, :, :].rearrange("p c m -> p (c m)"), T1[:, :]).then_inc(s_etok, 1)
                act.wait_ge(s_trc, u + 1)
                if not first:
                    act.wait_ge(s_okn, 6 * (u - 1) + 1)
                copy(c_inv[:, :, :].rearrange("p c m -> p (c m)"), T2[:, :]).then_inc(s_ctok, 1)
                if not last:
                    evac(ST, nu, ni)
                if tail and i >= 2:
                    norm_hi(i - 2, (0, 1), (T1, T2))
                projections, outputs = split_next(i, tail)
                if not last:
                    evac(VG0, nu, ni)
                if tail and i >= 2:
                    norm_hi(i - 2, (2, 3), (T1, T2))
                if not first:
                    out_hi(u - 1)
                act.wait_ge(s_okn, 6 * u + 3)
                act.activation(p[:, :], p[:, :], ACT.Exp).then_inc(s_exp, 1)
                if projections:
                    split_next_w(0, ST, nu)
                if not last:
                    evac(QT, nu, ni)
                    evac(VG1, nu, ni)
                if projections:
                    split_next_w(1, QT, nu)
                if outputs:
                    if not first:
                        act.wait_ge(s_y, CH * u)
                    split_o(0 if first else h_of[0] + 1, 0)
                if not last:
                    evac(KTJ, nu, ni)
                if projections:
                    split_next_w(2, KTJ, nu)
                if not last:
                    evac(VG2, nu, ni)
                if outputs:
                    split_o(0 if first else h_of[0] + 1, 1)
                if not first:
                    act.wait_ge(s_tro, 2 * u)
                    act.wait_ge(s_rstd, u)
                for k in range(2):
                    act.wait_ge(s_o, 2 * u + k + 1)
                    copy(o[:, 2 * k:2 * k + 2, :].rearrange("p a d -> p (a d)"), (T1, T3)[k][:, :]
                         ).then_inc(s_ocp, 1)
                    act.wait_ge(s_ocp, 2 * u + k + 1)
                    for c in (2 * k, 2 * k + 1):
                        for a in range(2):
                            at = (c % 2) * 2 * DV + a * DV
                            head = (T1, T3)[k][:, at:at + DV]
                            act.activation(head, head, ACT.Square,
                                           accum_out=ssq[:, 2 * c + a:2 * c + a + 1]).then_inc(s_sq, 1)
                if not last:
                    evac(VG3, nu, ni)

            h_of = [0]
            def token_hi(t):
                act.wait_ge(s_xtr, t + 1)
                copy(xh[:, :, t * P:(t + 1) * P],
                     (T0, T1)[t % 2][:, :].rearrange("p (k t) -> p k t", k=KT)).then_inc(s_xh, 1)

            split_w(0, wh["s"][:, :, :], 1)
            for t in range(CH):
                token_hi(t)
            for k in range(KT):
                split_vg(0, k)
            act.wait_ge(s_gn, 16)
            act.mul(half_gn[:, :], half_gn[:, :], 0.5).then_inc(s_gnh, 1)
            for j in range(JOBS):
                evac(j, 0, 0)
                if j < 2:
                    split_w(j + 1, wh["qk"[j]][:, :, :], j + 2)
                for t in tokens_after(j):
                    token_hi(t)
            act.wait_ge(s_gnh, 1)
            unit(0, 0)
            with act.Fori(0, PAIRS - 1) as h:
                h_of[0] = h
                for i in range(1, B + 1):
                    unit(h * B + i, i)
            for i in range(1, B):
                unit((PAIRS - 1) * B + i, i, last=(i == B - 1), tail=True)
            norm_hi(2, (0, 1), PJ)
            norm_hi(2, (2, 3), (T0, T2))
            out_hi(UNITS - 1)

        @block.gpsimd
        def _(pool):
            pool.memset(ident[:, :], 1.0).then_inc(s_const, 1)
            pool.wait_ge(s_const, 1)
            pool.affine_select(out=ident[:, :], in_=ident[:, :], compare_op=ALU.is_equal, fill=0.0, base=0,
                               pattern=[[1, P]], channel_multiplier=-1).then_inc(s_const, 1)
            pool.memset(tri[:, :], 1.0).then_inc(s_const, 1)
            pool.memset(neg_half[:, :], -0.5).then_inc(s_neg, 1)
            pool.wait_ge(s_neg, 1)
            pool.wait_ge(s_const, 3)
            pool.affine_select(out=tri[:, :], in_=tri[:, :], compare_op=ALU.is_ge, fill=0.0, base=0,
                               pattern=[[1, P]], channel_multiplier=-1).then_inc(s_const, 1)

            def lo(n, w_lo, w_hi, w):
                pool.wait_ge(s_wh, n)
                pool.tensor_tensor(w_lo, w, w_hi.bitcast(F32), ALU.subtract).then_inc(s_wl, 1)

            def lo_w(n, pair):
                name = "sqk"[n]
                lo(pair * 5 + n + 1, wl[name][:, :, :], wh[name][:, :, :],
                   stage[:, :].rearrange("p (k n) -> p k n", k=KT))

            def lo_vg(pair, k):
                pool.wait_ge(s_vgh, pair * KT + k + 1)
                pool.tensor_tensor(vgl[:, k, :], stage_vg[:, k, :], vgh[:, k, :].bitcast(F32), ALU.subtract
                                   ).then_inc(s_vgl2, 1)

            def unit(u, i, last=False, tail=False):
                projections, outputs = split_next(i, tail)
                first = isinstance(u, int) and u == 0
                if not first:
                    rsqrt(u - 1)
                if i == 3 and not tail:
                    pool.wait_ge(s_job, u * JOBS + VG3 + 1)
                    for k in range(2, KT):
                        lo_vg(h_of[0] + 1, k)
                if projections:
                    for n in range(3):
                        lo_w(n, h_of[0] + 1)
                if outputs:
                    pair = 0 if first else h_of[0] + 1
                    for a in range(2):
                        if not first:
                            pool.wait_ge(s_y, CH * u)
                        lo(pair * 5 + 4 + a, wol[:, a, :], woh[:, a, :], stage[:, :])

            def norm_rsqrt(b, n):
                pool.wait_ge(s_var, n + 1)
                pool.tensor_tensor(sd[b], sd[b], neg_half[:, 0:CH], ALU.pow).then_inc(s_sd, 1)

            def rsqrt(u):
                pool.wait_ge(s_ms, u + 1)
                if not (isinstance(u, int) and u == 0):
                    pool.wait_ge(s_og, u)
                pool.tensor_tensor(rstd[:, :], ssq[:, :], neg_half[:, :], ALU.pow).then_inc(s_rstd, 1)

            h_of = [0]
            norm_rsqrt(0, 0)
            lo_w(0, 0)
            norm_rsqrt(1, 1)
            for k in range(2, KT):
                lo_vg(0, k)
            norm_rsqrt(2, 2)
            lo_w(1, 0)
            norm_rsqrt(3, 3)
            lo_w(2, 0)
            unit(0, 0)
            with pool.Fori(0, PAIRS - 1) as h:
                h_of[0] = h
                for i in range(1, B + 1):
                    unit(h * B + i, i)
            for i in range(1, B):
                unit((PAIRS - 1) * B + i, i, last=(i == B - 1), tail=True)
                norm_rsqrt(i - 1, B + i - 1)
            rsqrt(UNITS - 1)

        @block.vector
        def _(dve):
            tri4 = tri[:, :].rearrange("p (c t) -> p c t", c=1).broadcast_to([P, CH, P])

            def lo(dst, src, hi):
                return dve.tensor_tensor(dst, src, hi.bitcast(F32), ALU.subtract)

            def lo_vg(pair, k):
                dve.wait_ge(s_vgh, pair * KT + k + 1)
                lo(vgl[:, k, :], stage_vg[:, k, :], vgh[:, k, :]).then_inc(s_vgl, 1)

            def clip(u, i):
                dve.wait_ge(s_job, u * JOBS + ST + 1)
                if not isinstance(u, int) or u >= 2:
                    dve.wait_ge(s_b, u - 1)
                dve.tensor_scalar(eT[i % 2][:, :], PJ[(JOBS * i + ST) % 2][:, :], -CLAMP, CLAMP,
                                  ALU.max, ALU.min).then_inc(s_clip, 1)

            def sums(u, i):
                dve.wait_ge(s_e, u + 1)
                if not isinstance(u, int) or u >= 2:
                    dve.wait_ge(s_trc, u - 1)
                dve.tensor_tensor_scan(cT[i % 2][:, :], eT[i % 2][:, :], eT[i % 2][:, :], 0.0, ALU.add,
                                       ALU.bypass).then_inc(s_scan, 1)
                dve.wait_ge(s_scan, u + 1)
                dve.reciprocal(cT[i % 2][:, :], cT[i % 2][:, :]).then_inc(s_cinv, 1)

            def gate(c, u, i):
                if not isinstance(u, int) or u >= 2:
                    dve.wait_ge(s_og, u - 1)
                dve.wait_ge(s_th, u * CH + c + 1)
                dve.scalar_tensor_tensor(out=g[i % 2][:, c, :], in0=th[:, :], scalar=1.0,
                                         in1=PJ[(JOBS * i + (VG0, VG1, VG2, VG3)[c]) % 2][:, 2 * DV:4 * DV],
                                         op0=ALU.add, op1=ALU.mult).then_inc(s_g, 1)

            def mask(u, s_in, s_out, used, count):
                dve.wait_ge(s_in, u + 1)
                if count is not None:
                    dve.wait_ge(used, count)
                for a in range(2):
                    dve.tensor_tensor(aT[:, a, :, :], A[a][:, :].rearrange("p (c t) -> p c t", c=CH), tri4,
                                      ALU.mult).then_inc(s_out, 1)

            def states(u, dst, width, parts, s_step):
                for c in range(CH - 1):
                    if c:
                        dve.wait_ge(s_step, u * 3 + c)
                    for a in range(2):
                        rows, cols = slice(64 * a, 64 * (a + 1)), slice(width * a, width * (a + 1))
                        src = parts(c)[rows, cols]
                        if c == 0:
                            st = dve.tensor_copy(dst[rows, c, cols], src)
                        else:
                            st = dve.tensor_tensor(dst[rows, c, cols], src, dst[rows, c - 1, cols], ALU.add)
                    st.then_inc(s_step, 1)

            def mean_square(u):
                dve.wait_ge(s_sq, 8 * (u + 1))
                dve.tensor_scalar(ssq[:, :], ssq[:, :], 1.0 / DV, EPS, ALU.mult, ALU.add).then_inc(s_ms, 1)

            def norm_gate(u, i):
                dve.wait_ge(s_rstd, u + 1)
                for c in range(CH):
                    for a in range(2):
                        blk = o[:, c, a * DV:(a + 1) * DV]
                        st = dve.scalar_tensor_tensor(out=blk, in0=blk, scalar=rstd[:, 2 * c + a:2 * c + a + 1],
                                                      in1=g[i % 2][:, c, a * DV:(a + 1) * DV],
                                                      op0=ALU.mult, op1=ALU.mult)
                st.then_inc(s_og, 1)

            def out_lo(u):
                for a in range(2):
                    dve.wait_ge(s_oh, 2 * u + a + 1)
                    if a == 0 and not (isinstance(u, int) and u == 0):
                        dve.wait_ge(s_y, CH * u)
                    lo(ol[:, a, :], A[a][:, :], oh[:, a, :]).then_inc(s_ol, 1)

            def add_y(u, i, c):
                dve.wait_ge(s_y, CH * u + c + 1)
                t = CH * (i % B) + c
                dve.tensor_tensor(y[:, t, :], y[:, t, :], (T2, A[0], A[1], T0)[c][:, :], ALU.add
                                  ).then_inc(s_ya, 1)

            def norm_statistics(b):
                dve.wait_ge(s_ya, CH * (UNITS - B + b + 1))
                if b == 0:
                    dve.wait_ge(s_fp8_out, 16 * (UNITS - B + 1))
                norm_stats(dve, y, b, stats[b], mv[b], sd[b], (s_mv, 2 * (B + b)), s_var)

            def norm_tokens(b, tiles):
                dve.wait_ge(s_sd, B + b + 1)
                for c in tiles:
                    t = CH * b + c
                    if t >= 2:
                        dve.wait_ge(s_ntr, t - 1)
                    dve.tensor_scalar(xn2[t % 2], y[:, t, :], mv[b][:, c, 0:1], sd[b][:, c:c + 1],
                                      ALU.subtract, ALU.mult).then_inc(s_n, 1)

            def norm_lo(b, tiles, banks):
                for c, src in zip(tiles, banks):
                    t = CH * b + c
                    dve.wait_ge(s_nh, t + 1)
                    cols = slice(t * P, (t + 1) * P)
                    lo(xl[:, :, cols], src[:, :].rearrange("p (k t) -> p k t", k=KT), xh[:, :, cols]
                       ).then_inc(s_nl, 1)

            def quantise(u, steps):
                n_q = QC0 if isinstance(u, int) else QC
                w, t = (q[:, :, 0:n_q] for q in (q8, q8t))
                todo = (
                    lambda: dve.tensor_scalar(t.bitcast(I32), w.bitcast(I32), 0x7F800000, None, ALU.bitwise_and),
                    lambda: dve.tensor_scalar(t, t, FP8_MIN_NORMAL, ROUNDER, ALU.max, ALU.mult),
                    lambda: dve.tensor_tensor(w, w, t, ALU.add),
                    lambda: dve.tensor_tensor(w, w, t, ALU.subtract),
                    lambda: dve.tensor_tensor(t, w, w, ALU.mult),
                    lambda: dve.tensor_scalar(t, t, FP8_MAX ** 2, FP8_MAX ** 2, ALU.max, ALU.subtract),
                    lambda: dve.tensor_scalar(t, t, HUGE, HUGE, ALU.mult, ALU.mult),
                    lambda: dve.scalar_tensor_tensor(out=w, in0=t, scalar=0.0, in1=w, op0=ALU.mult, op1=ALU.add))
                for n in range(Q8_STEPS)[steps]:
                    if n == 0:
                        dve.wait_ge(s_q8in, (u + 1) * 48)
                    else:
                        dve.wait_ge(s_q8, u * Q8_STEPS + n)
                    todo[n]().then_inc(s_q8, 1)

            def unit(u, i, last=False, tail=False):
                first = isinstance(u, int) and u == 0
                nu, ni = u + 1, i + 1
                if i == 3 and not tail:
                    dve.wait_ge(s_job, u * JOBS + VG3 + 1)
                    for k in range(2):
                        lo_vg(h_of[0] + 1, k)
                mask(u, s_a, s_am, s_o, None if first else 2 * u)
                if not first:
                    norm_gate(u - 1, i - 1)
                if not last:
                    clip(nu, ni)
                if tail and i >= 2:
                    norm_tokens(i - 2, (0, 1))
                dve.wait_ge(s_hkd, u + 1)
                if not first:
                    dve.wait_ge(s_ok, u)
                states(u, hk, DK, lambda c: T3[:, c * P:(c + 1) * P], s_hk)
                if tail and i >= 2:
                    norm_lo(i - 2, (0, 1), (T1, T2))
                    norm_tokens(i - 2, (2, 3))
                if not last:
                    sums(nu, ni)
                    gate(0, nu, ni)
                if tail and i >= 2:
                    norm_lo(i - 2, (2, 3), (T1, T2))
                k = [6 * u]

                def step(ins, wait=True):
                    k[0] += 1
                    ins.then_inc(s_okn, 1)
                    if wait:
                        dve.wait_ge(s_okn, k[0])

                p3 = p[:, :].rearrange("p (s m) -> p s m", m=M)
                dve.wait_ge(s_ok, u + 1)
                dve.wait_ge(s_ctok, u + 1)
                if not first:
                    dve.wait_ge(s_trw, u)
                step(dve.scalar_tensor_tensor(out=p[:, :], in0=T0[:, :], scalar=SCALE,
                                              in1=c_inv[:, :, :].rearrange("p c m -> p (c m)"),
                                              op0=ALU.mult, op1=ALU.mult))
                step(dve.tensor_reduce(mx[:, :], p3, AX.X, ALU.max))
                step(dve.tensor_tensor(p3, p3, mx[:, :].rearrange("p (s a) -> p s a", a=1).broadcast_to(
                    [P, 2 * CH, M]), ALU.subtract), wait=False)
                if not first:
                    out_lo(u - 1)
                dve.wait_ge(s_hvd, u + 1)
                if not first:
                    dve.wait_ge(s_o, 2 * u)
                states(u, hv, DV, lambda c: (T1[:, 0:256], T1[:, 256:512], T3[:, 0:256])[c], s_hv)
                dve.wait_ge(s_exp, u + 1)
                step(dve.tensor_reduce(sm[:, :], p3, AX.X, ALU.add))
                step(dve.reciprocal(rs[:, :], sm[:, :]))
                step(dve.tensor_tensor(p3, p3, rs[:, :].rearrange("p (s a) -> p s a", a=1).broadcast_to(
                    [P, 2 * CH, M]), ALU.mult), wait=False)
                if not first:
                    for c in range(CH):
                        add_y(u - 1, i - 1, c)
                dve.wait_ge(s_trw, u + 1)
                if not first:
                    dve.wait_ge(s_o, 2 * u)
                dve.tensor_tensor(wT[:, :], T2[:, :], cT[i % 2][:, :], ALU.mult).then_inc(s_wT, 1)
                if not last:
                    gate(1, nu, ni)
                if not tail:
                    quantise(u, slice(0, 5))
                mask(u, s_b, s_bm, s_ok, u + 1)
                if not tail:
                    quantise(u, slice(5, Q8_STEPS))
                if not last:
                    gate(2, nu, ni)
                if last:
                    norm_statistics(i - 1)
                mean_square(u)
                if not last:
                    gate(3, nu, ni)
                if tail and not last:
                    norm_statistics(i - 1)

            h_of = [0]
            dve.memset(hk[:, :, :], 0.0)
            dve.memset(hv[:, :, :], 0.0).then_inc(s_zero, 1)
            dve.wait_ge(s_zero, 1)

            def x_lo(t):
                dve.wait_ge(s_xh, t + 1)
                lo(xl[:, :, t * P:(t + 1) * P], (T0, T1)[t % 2][:, :].rearrange("p (k t) -> p k t", k=KT),
                   xh[:, :, t * P:(t + 1) * P]).then_inc(s_xl, 1)

            def token_stats(b):
                dve.wait_ge(s_x[b], 16)
                norm_stats(dve, y, b, stats[b], mv[b], sd[b], (s_mv, 2 * b), s_var)

            def token_norm(t):
                b, c = t // CH, t % CH
                dve.wait_ge(s_sd, b + 1)
                if t >= 2:
                    dve.wait_ge(s_xtr, t - 1)
                dve.tensor_scalar(o[:, 2 * (t % 2):2 * (t % 2) + 2, :].rearrange("p a d -> p (a d)"),
                                  y[:, t, :], mv[b][:, c, 0:1], sd[b][:, c:c + 1],
                                  ALU.subtract, ALU.mult).then_inc(s_xn, 1)

            token_stats(0)
            token_norm(0)
            token_norm(1)
            token_stats(1)
            x_lo(0)
            token_norm(2)
            x_lo(1)
            token_norm(3)
            x_lo(2)
            x_lo(3)
            for k in range(2):
                lo_vg(0, k)
            for j in range(JOBS):
                if j == ST:
                    clip(0, 0)
                elif j in (VG0, VG1, VG2, VG3):
                    gate((VG0, VG1, VG2, VG3).index(j), 0, 0)
                if j in (ST, QT):
                    token_stats(2 if j == ST else 3)
                if j == VG0:
                    sums(0, 0)
                for t in tokens_after(j):
                    token_norm(t)
                for t in tokens_after(j):
                    x_lo(t)
            dve.wait_ge(s_const, 4)
            unit(0, 0)
            with dve.Fori(0, PAIRS - 1) as h:
                h_of[0] = h
                for i in range(1, B + 1):
                    unit(h * B + i, i)
            for i in range(1, B):
                unit((PAIRS - 1) * B + i, i, last=(i == B - 1), tail=True)
            norm_tokens(2, (0, 1))
            norm_gate(UNITS - 1, B - 1)
            norm_lo(2, (0, 1), PJ)
            norm_tokens(2, (2, 3))
            norm_lo(2, (2, 3), (T0, T2))
            out_lo(UNITS - 1)
            for c in range(CH):
                add_y(UNITS - 1, B - 1, c)


def feed_forward(nc, sb_top, sem, fp8_scratch, gate_s, up_s, down_s, out, shared):
    y, ident, bank, xh, xl, wg0, wu0, neg_half, s_early = shared
    Y = bank[4:8]
    NB = B - 1
    with ExitStack() as ctx:
        def sb(name, shape, dt=F32):
            return sb_top(name, shape, dt, ctx)

        wg, wu = (sb(n, [P, KT, F - EARLY * P], F32R) for n in ("w_gate", "w_up"))
        wd = sb("w_down", [P, FT, D], F32R)
        xn = sb("xn", [P, CH, D])
        gs, us = sb("gate_scale", [P, FT]), sb("up_scale", [P, FT])
        hgs, gus = sb("half_gate_scale", [P, FT]), sb("half_gate_up_scale", [P, FT])
        ds_row = sb("down_scale", [P, D])
        th, ga = (sb(n, [P, 2, T]) for n in ("tanh_half", "gated"))
        fh, fl = (sb(n, [P, 2, T], F32R) for n in ("fuse_hi", "fuse_lo"))
        res = sb("result", [P, CH, D])
        stats = sb("stats2", [P, CH, 6])
        mv = sb("mean_var2", [P, CH, 2])
        sd = sb("ln_rstd2", [P, CH])

        PARTS = FT // EARLY
        s_wgu = [sem(f"gate_up_loaded{n}") for n in range(PARTS)]
        s_wd = [sem(f"down_loaded{n}") for n in range(PARTS)]
        s_sc = sem("ffn_scales_loaded")
        s_hgs, s_gus = sem("half_scale_ready"), sem("scale_product_ready")
        s_mv, s_var, s_sd = sem("n3_stats_step"), sem("n3_var_ready"), sem("n3_sd_ready")
        s_xn, s_xtr, s_xh, s_xl = sem("n3_ready"), sem("n3_transposed"), sem("n3T_hi_ready"), sem("n3T_lo_ready")
        s_gu, s_th, s_ga, s_fu = sem("gate_up_done"), sem("tanh2_ready"), sem("gated_ready"), sem("fuse_ready")
        s_fh, s_fl, s_dn = sem("fuse_hi_ready"), sem("fuse_lo_ready"), sem("down_done")
        s_ys, s_res, s_out = sem("y_scaled"), sem("result_ready"), sem("result_stored")

        block = ctx.enter_context(nc.Block())

        def blocks(eng, tokens):
            tokens(0, first=True)
            with eng.Fori(1, B - 1) as b:
                tokens(b)
            tokens(B - 1, last=True)

        @block.sync
        def _(sp):
            with nc.allow_non_contiguous_dma(reason="per-feature scales, once"):
                sp.dma_start(gs[:, :], gate_s.rearrange("(f p) -> p f", p=P)).then_inc(s_sc, 16)
                sp.dma_start(us[:, :], up_s.rearrange("(f p) -> p f", p=P)).then_inc(s_sc, 16)
            down = fp8_scratch[2].rearrange("p c -> (p c)").rearrange("(k q n) -> q k n", k=FT, q=P)
            for n in range(PARTS):
                f0, f1 = n * EARLY, (n + 1) * EARLY
                if n:
                    for m, w in enumerate((wg, wu)):
                        sp.dma_start(w[:, :, (f0 - EARLY) * P:(f1 - EARLY) * P].bitcast(F32),
                                     gate_up_columns(fp8_scratch[m], KT, f0, f1)).then_inc(s_wgu[n], 16)
                sp.dma_start(wd[:, f0:f1, :].bitcast(F32), down[:, f0:f1, :]).then_inc(s_wd[n], 16)
                if n == 0:
                    sp.dma_start(ds_row[:, :], down_s.rearrange("(a n) -> a n", a=1).broadcast_to([P, D])
                                 ).then_inc(s_sc, 16)
            with sp.Fori(0, B) as b:
                for c in range(CH):
                    sp.wait_ge(s_res, b * CH + c + 1)
                    sp.dma_start(out.rearrange("b (c p) d -> (b c) p d", p=P)[bass.ds(b * CH + c, 1), :, :]
                                 .rearrange("a p d -> (a p) d"), res[:, c, :]).then_inc(s_out, 16)
            sp.wait_ge(s_out, 16 * TILES)

        @block.gpsimd
        def _(pool):
            pool.wait_ge(s_var, 1)
            pool.tensor_tensor(sd[:, :], sd[:, :], neg_half[:, 0:CH], ALU.pow).then_inc(s_sd, 1)

        @block.tensor
        def _(pe):
            def gate_up(b, f, first):
                if not (first and f < 2):
                    pe.wait_ge(s_fu, b * FT + f - 1)
                if first and f % EARLY == 0:
                    if f:
                        pe.wait_ge(s_wgu[f // EARLY], 32)
                    else:
                        pe.wait_ge(s_early, 32)
                at = (f if f < EARLY else f - EARLY) * P
                for w, dst in (((wg0, wu0) if f < EARLY else (wg, wu))[0], bank[2 * (f % 2)]), \
                              (((wg0, wu0) if f < EARLY else (wg, wu))[1], bank[2 * (f % 2) + 1]):
                    for k in range(KT):
                        for part in (xh, xl):
                            mm = pe.matmul(dst[:, :], w[:, k, at:at + P], part[:, k, bass.ds(b * T, T)],
                                           start=(k == 0 and part is xh), stop=(k == KT - 1 and part is xl))
                mm.then_inc(s_gu, 1)

            def tokens(b, first=False, last=False):
                for f in range(FT):
                    if f + 1 < FT:
                        gate_up(b, f + 1, first)
                    elif not last:
                        gate_up(b + 1, 0, False)
                    if first and f == 0:
                        for c in range(CH):
                            pe.wait_ge(s_xn, c + 1)
                            for k in range(KT):
                                mm = pe.transpose(Y[c][:, k * P:(k + 1) * P], xn[:, c, k * P:(k + 1) * P],
                                                  ident[:, :])
                            mm.then_inc(s_xtr, 1)
                        pe.wait_ge(s_xl, CH)
                    pe.wait_ge(s_fh, b * FT + f + 1)
                    pe.wait_ge(s_fl, b * FT + f + 1)
                    if first and f % EARLY == 0:
                        pe.wait_ge(s_wd[f // EARLY], 16)
                    for c in range(CH):
                        if f == 0 and not first:
                            pe.wait_ge(s_ys, (b - 1) * CH + c + 1)
                        for part in (fh, fl):
                            mm = pe.matmul(Y[c][:, :], part[:, f % 2, c * P:(c + 1) * P], wd[:, f, :],
                                           start=(f == 0 and part is fh), stop=(f == FT - 1 and part is fl))
                    mm.then_inc(s_dn, 1)

            gate_up(0, 0, True)
            blocks(pe, tokens)

        @block.scalar
        def _(act):
            act.wait_ge(s_sc, 48)
            act.mul(hgs[:, :], gs[:, :], 0.5).then_inc(s_hgs, 1)
            act.wait_ge(s_hgs, 1)

            def feature(b, f, early):
                act.wait_ge(s_gu, b * FT + f + 1)
                if not early:
                    act.wait_ge(s_ga, b * FT + f - 1)
                act.activation(th[:, f % 2, :], bank[2 * (f % 2)][:, :], ACT.Tanh, scale=hgs[:, f:f + 1]
                               ).then_inc(s_th, 1)
                act.wait_ge(s_fu, b * FT + f + 1)
                if not early:
                    act.wait_ge(s_dn, b * FT + f - 1)
                act.activation(fh[:, f % 2, :], ga[:, f % 2, :], ACT.Copy).then_inc(s_fh, 1)

            def tokens(b, first=False, last=False):
                for f in range(FT):
                    feature(b, f, first and f < 2)
                    if first and f == 0:
                        for c in range(CH):
                            act.wait_ge(s_xtr, c + 1)
                            t = NB * CH + c
                            act.activation(xh[:, :, t * P:(t + 1) * P],
                                           Y[c][:, :].rearrange("p (k t) -> p k t", k=KT), ACT.Copy
                                           ).then_inc(s_xh, 1)

            blocks(act, tokens)

        @block.vector
        def _(dve):
            norm_stats(dve, y, NB, stats, mv, sd[:, :], (s_mv, 0), s_var)
            dve.wait_ge(s_hgs, 1)
            dve.tensor_tensor(gus[:, :], hgs[:, :], us[:, :], ALU.mult).then_inc(s_gus, 1)
            dve.wait_ge(s_sd, 1)
            for c in range(CH):
                dve.tensor_scalar(xn[:, c, :], y[:, NB * CH + c, :], mv[:, c, 0:1], sd[:, c:c + 1],
                                  ALU.subtract, ALU.mult).then_inc(s_xn, 1)
            dve.wait_ge(s_gus, 1)

            def fuse(b, f, early):
                dve.wait_ge(s_th, b * FT + f + 1)
                if not early:
                    dve.wait_ge(s_fl, b * FT + f - 1)
                    dve.wait_ge(s_fh, b * FT + f - 1)
                dve.scalar_tensor_tensor(out=ga[:, f % 2, :], in0=th[:, f % 2, :], scalar=1.0,
                                         in1=bank[2 * (f % 2)][:, :], op0=ALU.add, op1=ALU.mult
                                         ).then_inc(s_ga, 1)
                dve.wait_ge(s_ga, b * FT + f + 1)
                dve.scalar_tensor_tensor(out=ga[:, f % 2, :], in0=ga[:, f % 2, :], scalar=gus[:, f:f + 1],
                                         in1=bank[2 * (f % 2) + 1][:, :], op0=ALU.mult, op1=ALU.mult
                                         ).then_inc(s_fu, 1)
                dve.wait_ge(s_fh, b * FT + f + 1)
                dve.tensor_tensor(fl[:, f % 2, :], ga[:, f % 2, :], fh[:, f % 2, :].bitcast(F32),
                                  ALU.subtract).then_inc(s_fl, 1)

            def scale(b, first):
                dve.wait_ge(s_dn, b * FT + FT)
                for c in range(CH):
                    if not first:
                        dve.wait_ge(s_out, b * 16 * CH)
                    dve.tensor_tensor(res[:, c, :], Y[c][:, :], ds_row[:, :], ALU.mult).then_inc(s_ys, 1)

            def residual(b, first):
                for c in range(CH):
                    dve.wait_ge(s_ys, b * CH + c + 1)
                    dve.tensor_tensor(res[:, c, :], res[:, c, :],
                                      y[:, c, :] if first else y[:, bass.ds(b * CH + c, 1), :].rearrange(
                                          "p a d -> p (a d)"), ALU.add).then_inc(s_res, 1)

            def tokens(b, first=False, last=False):
                for f in range(2, FT):
                    fuse(b, f, False)
                if not last:
                    fuse(b + 1, 0, False)
                scale(b, first)
                if not last:
                    fuse(b + 1, 1, False)
                residual(b, first)

            fuse(0, 0, True)
            for c in range(CH):
                dve.wait_ge(s_xh, c + 1)
                cols = slice((NB * CH + c) * P, (NB * CH + c + 1) * P)
                dve.tensor_tensor(xl[:, :, cols], Y[c][:, :].rearrange("p (k t) -> p k t", k=KT),
                                  xh[:, :, cols].bitcast(F32), ALU.subtract).then_inc(s_xl, 1)
            fuse(0, 1, True)
            blocks(dve, tokens)


_INS = ["L0_attn_hidden_states", "L0_attn_Wq", "L0_attn_Wk", "L0_attn_Wv", "L0_attn_Wg", "L0_attn_Ws",
        "L0_attn_Wo", "L0_attn_g_norm_weight", "L0_ffn_gate_w", "L0_ffn_up_w", "L0_ffn_down_w",
        "L0_ffn_gate_scale", "L0_ffn_up_scale", "L0_ffn_down_scale"]


def kernel(**inputs):
    import numpy as _np
    import concourse.bacc as _bacc
    from concourse import mybir as _mybir
    from concourse.bass_utils import run_bass_kernel_spmd as _run

    nc = _bacc.Bacc("TRN2", target_bir_lowering=False, num_devices=1)
    arrays, args = {}, []
    for name in _INS:
        a = _np.ascontiguousarray(inputs[name])
        arrays[f"in_{name}"] = a
        args.append(nc.dram_tensor(f"in_{name}", a.shape, _mybir.dt.from_np(a.dtype), kind="ExternalInput").ap())
    args.append(nc.dram_tensor("out_0", (B, T, D), F32, kind="ExternalOutput").ap())
    gsa_swiglu(nc, *args)
    r = _run(nc, [arrays], core_ids=[0])
    return r.results[0]["out_0"]
```

```python
from contextlib import ExitStack

import concourse.bass as bass
from concourse import mybir
from concourse.alu_op_type import AluOpType as ALU

F32 = mybir.dt.float32
F32R = mybir.dt.float32r
I32 = mybir.dt.int32
ACT = mybir.ActivationFunctionType
AX = mybir.AxisListType

P = 128
B, T, D = 4, 512, 512
H, DK, DV, M = 16, 64, 128, 64
F = 1536
KT = D // P
CH = T // P
PAIRS = H // 2
UNITS = PAIRS * B
TILES = B * CH
FT = F // P
EPS = 1e-5
CLAMP = 32.0
SCALE = DK ** -0.5
FP8_MAX = 448.0
FP8_MIN_NORMAL = 2.0 ** -6
ROUNDER = 1.5 * 2.0 ** 20
HUGE = 3.0e38
Q8_STEPS = 8
QF = D * F // P
QC = 212
QC0 = QF - QC * (UNITS - B)
assert 0 < QC0 <= QC
EARLY = 4

ST, VG0, QT, VG1, KTJ, VG2, VG3 = range(7)
JOBS = 7


def gsa_swiglu(nc, x, Wq, Wk, Wv, Wg, Ws, Wo, gnorm, gate_w, up_w, down_w, gate_s, up_s, down_s, out):
    fp8_scratch = nc.dram_tensor("fp8_weights", (3, P, QF), F32, kind="Internal").ap()
    flat = [w.rearrange("a b -> (a b)").rearrange("(p c) -> p c", p=P) for w in (gate_w, up_w, down_w)]

    top = ExitStack()
    with top:
        def sb(name, shape, dt=F32, ctx=top):
            return ctx.enter_context(nc.sbuf_tensor(name, shape, dt))

        def sem(name):
            return top.enter_context(nc.semaphore(name))

        y = sb("y", [P, TILES, D])
        ident = sb("ident", [P, P])
        bank = [top.enter_context(nc.psum_tensor(f"bank{i}", [P, 512], F32)) for i in range(8)]

        xh, xl = (sb(n, [P, KT, B * T], F32R) for n in ("xT_hi", "xT_lo"))
        vgh, vgl = (sb(n, [P, KT, 2 * 2 * DV], F32R) for n in ("wvg_hi", "wvg_lo"))
        neg_half = sb("neg_half", [P, 2 * CH])

        mx, sm = sb("slot_max", [P, 2 * CH]), sb("slot_sum", [P, 2 * CH])
        last_mv, last_sd = mx[:, :].rearrange("p (t s) -> p t s", s=2), sm[:, 0:CH]

        gs, us = sb("gate_scale", [P, FT]), sb("up_scale", [P, FT])

        s_early = [sem("early_gate_loaded"), sem("early_up_loaded")]
        s_gu = sem("gate_up_done")
        shared = (y, ident, bank, xh, xl, vgh, vgl, neg_half, mx, sm, last_mv, last_sd, gs, us,
                  s_early, s_gu)
        attention(nc, sb, sem, x, Wq, Wk, Wv, Wg, Ws, Wo, gnorm, flat, gate_s, up_s, fp8_scratch, shared)
        feed_forward(nc, sb, sem, fp8_scratch, down_s, out, shared)


def gate_up_columns(scratch, k_tiles, f0, f1):
    return scratch.rearrange("p c -> (p c)").rearrange("(k q n) -> q k n", k=k_tiles, q=P)[:, :, f0 * P:f1 * P]


def gate_up_product(pe, dst, w, at, xh, xl, b):
    for k in range(KT):
        for part in (xh, xl):
            mm = pe.matmul(dst[:, :], w[:, k, at:at + P], part[:, k, bass.ds(b * T, T)],
                           start=(k == 0 and part is xh), stop=(k == KT - 1 and part is xl))
    return mm


def norm_stats(dve, y, b, stats, mv, sd, s_step, s_var, ready=None, tiles=range(CH)):
    for c in tiles:
        if ready:
            dve.wait_ge(*ready[c])
        st = dve.bn_stats(stats[:, c, :], y[:, CH * b + c, :])
    st.then_inc(s_step[0], 1)
    norm_aggregate(dve, stats, mv, sd, s_step, s_var, tiles)


def norm_aggregate(dve, stats, mv, sd, s_step, s_var, tiles=range(CH)):
    dve.wait_ge(s_step[0], s_step[1] + 1)
    for c in tiles:
        st = dve.bn_aggr(mv[:, c, :], stats[:, c, :])
    st.then_inc(s_step[0], 1)
    dve.wait_ge(s_step[0], s_step[1] + 2)
    cols = slice(tiles[0], tiles[-1] + 1)
    dve.tensor_scalar(sd[:, cols], mv[:, cols, 1], EPS, None, ALU.add).then_inc(s_var, 1)


def attention(nc, sb_top, sem, x, Wq, Wk, Wv, Wg, Ws, Wo, gnorm, flat, gate_s, up_s, fp8_scratch, shared):
    y, ident, bank, xh, xl, vgh, vgl, neg_half, mx, sm, last_mv, last_sd, gs, us, s_early, s_gu = shared
    PJ, A, (T0, T1, T2, T3) = bank[0:2], bank[2:4], bank[4:8]

    with ExitStack() as ctx:
        def sb(name, shape, dt=F32):
            return sb_top(name, shape, dt, ctx)

        wh = {n: sb(f"w{n}_hi", [P, KT, P], F32R) for n in "sqk"}
        wl = {n: sb(f"w{n}_lo", [P, KT, P], F32R) for n in "sqk"}
        woh, wol = (sb(n, [P, 2, D], F32R) for n in ("wo_hi", "wo_lo"))
        stage = sb("stage", [P, D])
        stage_vg = sb("stage_vg", [P, KT, 4 * DV])

        qT, kT = sb("qT", [P, T]), sb("kT", [P, T])
        k_tok, e_tok, c_inv = (sb(n, [P, CH, P]) for n in ("k_tok", "e_tok", "c_inv"))
        eT = [sb(f"eT{i}", [P, T]) for i in range(2)]
        cT = [sb(f"cT{i}", [P, T]) for i in range(2)]
        v = [sb(f"v{i}", [P, CH, 2 * DV]) for i in range(2)]
        g = [sb(f"g{i}", [P, CH, 2 * DV]) for i in range(2)]
        th = sb("tanh_half_g", [P, 2 * DV])
        aT = sb("aT", [P, 2, CH, P])
        hk = sb("hk", [P, CH - 1, P])
        hv = sb("hv", [P, CH - 1, 2 * DV])
        p = sb("p", [P, CH * P])
        wT = sb("wT", [P, T])
        o = sb("o", [P, CH, 2 * DV])
        oh, ol = (sb(n, [P, 2, T], F32R) for n in ("oT_hi", "oT_lo"))
        q8 = sb("q8", [P, 3, QC])
        q8t = sb("q8t", [P, 3, QC])
        tri = sb("tri", [P, P])
        half_gn = sb("half_gn", [P, 1])
        ssq, rstd = sb("ssq", [P, 2 * CH]), sb("rstd", [P, 2 * CH])
        rs = sb("slot_rsum", [P, 2 * CH])
        q8_flat, q8t_flat = (q[:, :, :].rearrange("p a b -> p (a b)") for q in (q8, q8t))
        xn2 = [q[:, 0:D] for q in (q8_flat, q8t_flat)]

        def norm_tile(t):
            return (eT[0][:, :], cT[0][:, :])[t % 2] if t in (2 * CH + 2, 2 * CH + 3) else xn2[t % 2]

        stats = [q8_flat[:, D + 24 * b:D + 24 * (b + 1)].rearrange("p (t s) -> p t s", s=6) for b in range(B)]
        mv = [q8t_flat[:, D + 8 * b:D + 8 * (b + 1)].rearrange("p (t s) -> p t s", s=2) for b in range(B)]
        sd = [q8t_flat[:, D + 32 + CH * b:D + 32 + CH * (b + 1)] for b in range(B)]

        s_const = sem("const_ready")
        s_x0, s_x = [sem(f"x0_loaded{c}") for c in range(CH)], [None] + [sem(f"x_loaded{b}") for b in range(1, B)]
        s_fp8_out = sem("fp8_stored")
        s_gn, s_sc = sem("gnorm_loaded"), sem("gate_up_scales_loaded")
        s_hgs = sem("half_gate_scale_ready")
        s_last_var = sem("last_var_ready")
        s_mv, s_var = sem("ln_stats_step"), sem("ln_var_ready")
        s_n, s_ntr = sem("n_ready"), sem("n_transposed")
        s_nh, s_nl = sem("nT_hi_ready"), sem("nT_lo_ready")
        s_sd = sem("ln_sd_ready")
        s_neg = sem("exponent_ready")
        s_zero, s_gnh = sem("states_zeroed"), sem("half_gnorm_ready")
        s_xn = sem("ln_x_ready")
        s_xtr = sem("ln_x_transposed")
        s_xh, s_xl = sem("xT_hi_ready"), sem("xT_lo_ready")
        s_stage, s_stage_vg = sem("stage_loaded"), [sem(f"stage_vg_loaded{k}") for k in range(KT)]
        s_wh, s_wl = sem("w_hi_ready"), sem("w_lo_ready")
        s_vgh = sem("vg_hi_ready")
        s_vgl, s_vgl2 = sem("vg_lo_ready"), sem("vg_lo_2_ready")
        s_wos = sem("wo_scaled")
        s_job = sem("job_done")
        s_clip, s_q, s_k, s_e = sem("s_clipped"), sem("q_ready"), sem("k_ready"), sem("e_ready")
        s_scan, s_cinv = sem("c_summed"), sem("c_inverted")
        s_v, s_th, s_g = sem("v_ready"), sem("tanh_ready"), sem("g_ready")
        s_trk, s_tre, s_trc = sem("k_transposed"), sem("e_transposed"), sem("c_transposed")
        s_ktok, s_etok, s_ctok = sem("k_tok_ready"), sem("e_tok_ready"), sem("c_inv_ready")
        s_a, s_am = sem("scores_done"), sem("scores_masked")
        s_hkd, s_hk = sem("hk_parts_done"), sem("hk_step")
        s_hvd, s_hv = sem("hv_parts_done"), sem("hv_step")
        s_ok, s_okn = sem("ok_done"), sem("softmax_step")
        s_exp = sem("slot_exp_ready")
        s_trw, s_wT = sem("w_transposed"), sem("wT_ready")
        s_b, s_bm = sem("value_weights_done"), sem("value_weights_masked")
        s_o, s_ocp, s_sq = sem("o_done"), sem("o_copied"), sem("o_squared")
        s_ms, s_rstd, s_og = sem("o_mean_square"), sem("o_rstd_ready"), sem("o_gated")
        s_tro, s_oh, s_ol = sem("o_transposed"), sem("oT_hi_ready"), sem("oT_lo_ready")
        s_y, s_ya = sem("y_done"), sem("y_added")
        s_q8in, s_q8 = sem("fp8_in_loaded"), sem("fp8_step")

        block = ctx.enter_context(nc.Block())

        def tokens_after(j):
            b = {VG0: 1, VG1: 2, VG2: 3}.get(j, B)
            return range(CH * b, min(CH * (b + 1), TILES))

        def token_tile(t):
            if t % 4 < 2:
                return o[:, 2 * (t % 4):2 * (t % 4) + 2, :].rearrange("p a d -> p (a d)")
            return aT[:, t % 4 - 2, :, :].rearrange("p c t -> p (c t)")

        def split_next(i, tail):
            return i == 2 and not tail, i in (0, B)

        @block.sync
        def _(sp):
            def load_x(b):
                if b == 0:
                    for c in range(CH):
                        sp.dma_start(y[:, c, :], x[0, P * c:P * (c + 1), :]).then_inc(s_x0[c], 16)
                    return
                sp.dma_start(y[:, CH * b:CH * (b + 1), :],
                             x[b].rearrange("(c p) d -> p c d", p=P)).then_inc(s_x[b], 16)

            load_x(0)
            sp.dma_start(half_gn[:, :], gnorm.rearrange("(p a) -> p a", a=1)).then_inc(s_gn, 16)

            def load_sqk(pair, n):
                if not (isinstance(pair, int) and n == 0):
                    sp.wait_ge(s_wl, pair * 5 + n)
                sp.dma_start(stage[:, :].rearrange("p (k n) -> p k n", k=KT),
                             (Ws, Wq, Wk)[n].rearrange("(k p) n -> p k n", p=P)[:, :, bass.ds(pair * P, P)]
                             ).then_inc(s_stage, 16)

            def load_vg(pair):
                for k in range(KT):
                    if not isinstance(pair, int):
                        sp.wait_ge((s_vgl, s_vgl2)[k // 2], (pair - 1) * 2 + k % 2 + 1)
                    for n, w in enumerate((Wv, Wg)):
                        sp.dma_start(stage_vg[:, k, n * 2 * DV:(n + 1) * 2 * DV],
                                     w[P * k:P * (k + 1), bass.ds(pair * 2 * DV, 2 * DV)]
                                     ).then_inc(s_stage_vg[k], 16)

            def load_o(pair, a):
                sp.wait_ge(s_wl, pair * 5 + 3 + a)
                sp.dma_start(stage[:, :], Wo[bass.ds(pair * 2 * DV + a * DV, DV), :]).then_inc(s_stage, 16)

            def slice_of(u):
                return (0, QC0) if isinstance(u, int) else ((u - 1) * QC + QC0, QC)

            def load_q8(u):
                if isinstance(u, int):
                    sp.wait_ge(s_xn, TILES)
                else:
                    sp.wait_ge(s_fp8_out, 16 * u)
                start, n = slice_of(u)
                for m, w in enumerate(flat):
                    sp.dma_start(q8[:, m, 0:n], w[:, bass.ds(start, n)]).then_inc(s_q8in, 16)

            def store_q8(u):
                sp.wait_ge(s_q8, Q8_STEPS * (u + 1))
                start, n = slice_of(u)
                sp.dma_start(fp8_scratch[:, :, bass.ds(start, n)].rearrange("n p c -> p n c"),
                             q8[:, :, 0:n]).then_inc(s_fp8_out, 16)

            load_sqk(0, 0)
            load_vg(0)
            load_x(1)
            load_sqk(0, 1)
            load_x(2)
            load_x(3)
            load_sqk(0, 2)
            with nc.allow_non_contiguous_dma(reason="per-feature scales, once"):
                for tile, scale in ((gs, gate_s), (us, up_s)):
                    sp.dma_start(tile[:, :], scale.rearrange("(f p) -> p f", p=P)).then_inc(s_sc, 16)
            load_o(0, 0)
            load_q8(0)
            load_o(0, 1)
            store_q8(0)
            with sp.Fori(0, PAIRS - 1) as h:
                for i in range(1, B + 1):
                    load_q8(h * B + i)
                    if i == 1:
                        load_sqk(h + 1, 0)
                        load_vg(h + 1)
                    if i == 2:
                        load_sqk(h + 1, 1)
                        load_sqk(h + 1, 2)
                        load_o(h + 1, 0)
                    if i == B:
                        load_o(h + 1, 1)
                    store_q8(h * B + i)
            sp.wait_ge(s_fp8_out, 16 * (UNITS - B + 1))
            sp.wait_ge(s_job, JOBS * UNITS)
            for n, w in enumerate((vgh, vgl)):
                sp.dma_start(w[:, :, :].bitcast(F32), gate_up_columns(fp8_scratch[n], KT, 0, EARLY)
                             ).then_inc(s_early[n], 16)

        @block.tensor
        def _(pe):
            def product3(dst, pairs):
                n = len(pairs)
                for k, (w_hi, w_lo, m_hi, m_lo) in enumerate(pairs):
                    pe.matmul(dst, w_hi, m_hi, start=(k == 0), stop=False)
                    pe.matmul(dst, w_hi, m_lo, start=False, stop=False)
                    last = pe.matmul(dst, w_lo, m_hi, start=False, stop=(k == n - 1))
                return last

            def job(j, u, i):
                b = i % B
                dst = PJ[(JOBS * i + j) % 2]
                first = isinstance(u, int) and u == 0
                if j == ST:
                    if not first:
                        pe.wait_ge(s_v, u * CH - 1)
                        pe.wait_ge(s_g, u * CH - 1)
                    if b == 0:
                        pe.wait_ge(s_wl, 5 * pair_of(u, i) + 1)
                    if not isinstance(u, int) or u < B:
                        pe.wait_ge(s_xl, CH * (b + 1))
                elif j == VG0:
                    if not first:
                        pe.wait_ge(s_v, u * CH)
                        pe.wait_ge(s_g, u * CH)
                    if b == 0:
                        pe.wait_ge(s_vgl, 2 * pair_of(u, i) + 2)
                        pe.wait_ge(s_vgl2, 2 * pair_of(u, i) + 2)
                elif j == QT:
                    pe.wait_ge(s_clip, u + 1)
                    if b == 0:
                        pe.wait_ge(s_wl, 5 * pair_of(u, i) + 2)
                elif j == VG1:
                    pe.wait_ge(s_v, u * CH + 1)
                    pe.wait_ge(s_g, u * CH + 1)
                elif j == KTJ:
                    pe.wait_ge(s_q, u + 1)
                    if b == 0:
                        pe.wait_ge(s_wl, 5 * pair_of(u, i) + 3)
                elif j == VG2:
                    pe.wait_ge(s_v, u * CH + 2)
                    pe.wait_ge(s_g, u * CH + 2)
                elif j == VG3:
                    pe.wait_ge(s_k, u + 1)
                if j in (ST, QT, KTJ):
                    n = {ST: "s", QT: "q", KTJ: "k"}[j]
                    cols = slice(T * b, T * (b + 1))
                    last = product3(dst[:, :], [(wh[n][:, k, :], wl[n][:, k, :], xh[:, k, cols], xl[:, k, cols])
                                                for k in range(KT)])
                else:
                    c = {VG0: 0, VG1: 1, VG2: 2, VG3: 3}[j]
                    cols = slice(T * b + P * c, T * b + P * (c + 1))
                    last = product3(dst[:, :], [(xh[:, k, cols], xl[:, k, cols], vgh[:, k, :], vgl[:, k, :])
                                                for k in range(KT)])
                last.then_inc(s_job, 1)

            def pair_of(u, i):
                return u // B if isinstance(u, int) else pair_reg[0] + i // B

            pair_reg = [None]

            def out_transposes(u, banks=A):
                pe.wait_ge(s_og, u + 1)
                if banks is A:
                    pe.wait_ge(s_am, 2 * (u + 1) + 2)
                else:
                    pe.wait_ge(s_nl, 3 * CH)
                for a in range(2):
                    for c in range(CH):
                        last = pe.transpose(banks[a][:, c * P:(c + 1) * P], o[:, c, a * DV:(a + 1) * DV],
                                            ident[:, :])
                    last.then_inc(s_tro, 1)

            def out_product(u, pair_ready, banks=A):
                pe.wait_ge(s_oh, 2 * (u + 1))
                pe.wait_ge(s_ol, 2 * (u + 1))
                if pair_ready is not None:
                    pe.wait_ge(s_wl, pair_ready)
                for c, dst in enumerate((T2, banks[0], banks[1], T0)):
                    if c == 3 and banks is A:
                        pe.wait_ge(s_okn, 6 * (u + 1) + 1)
                    cols = slice(c * P, (c + 1) * P)
                    product3(dst[:, :], [(oh[:, a, cols], ol[:, a, cols], woh[:, a, :], wol[:, a, :])
                                         for a in range(2)]).then_inc(s_y, 1)

            def unit(u, i, last=False, tail=False):
                par = i % 2
                first = isinstance(u, int) and u == 0
                nu, ni = u + 1, i + 1
                pe.wait_ge(s_k, u + 1)
                if not first:
                    pe.wait_ge(s_okn, 6 * (u - 1) + 1)
                for c in range(CH):
                    mm = pe.transpose(T0[:, c * P:(c + 1) * P], kT[:, c * P:(c + 1) * P], ident[:, :])
                mm.then_inc(s_trk, 1)
                pe.wait_ge(s_q, u + 1)
                if not first:
                    pe.wait_ge(s_bm, 2 * u)
                for c in range(CH):
                    for a in range(2):
                        hs, cs = slice(DK * a, DK * (a + 1)), slice(c * P, (c + 1) * P)
                        mm = pe.matmul(A[a][:, cs], kT[hs, cs], qT[hs, cs], start=True, stop=True)
                mm.then_inc(s_a, 1)
                pe.wait_ge(s_e, u + 1)
                if not first:
                    pe.wait_ge(s_sq, 2 * CH * u)
                for c in range(CH):
                    mm = pe.transpose(T1[:, c * P:(c + 1) * P], eT[par][:, c * P:(c + 1) * P], ident[:, :])
                mm.then_inc(s_tre, 1)
                if first:
                    job(ST, nu, ni)
                pe.wait_ge(s_cinv, u + 1)
                if not first:
                    pe.wait_ge(s_wT, u)
                for c in range(CH):
                    mm = pe.transpose(T2[:, c * P:(c + 1) * P], cT[par][:, c * P:(c + 1) * P], ident[:, :])
                mm.then_inc(s_trc, 1)
                if not last and not first:
                    job(ST, nu, ni)
                if tail and i >= 2:
                    norm_transposes(i - 2, (0, 1), (T1, T2))
                pe.wait_ge(s_ktok, u + 1)
                pe.wait_ge(s_etok, u + 1)
                for c in range(CH - 1):
                    mm = pe.matmul(T3[:, c * P:(c + 1) * P], k_tok[:, c, :], e_tok[:, c, :], start=True, stop=True)
                mm.then_inc(s_hkd, 1)
                if not last:
                    job(VG0, nu, ni)
                else:
                    pe.wait_ge(s_g, CH * UNITS)
                    early_product(0, 0)
                if tail and i >= 2 and not last:
                    pe.wait_ge(s_nl, CH * (i - 2) + 2)
                    norm_transposes(i - 2, (2, 3), (T1, T2))
                pe.wait_ge(s_am, 2 * u + 2)
                pe.wait_ge(s_hk, 3 * (u + 1))
                for c in range(CH):
                    if c:
                        pe.matmul(T0[:, c * P:(c + 1) * P], qT[:, c * P:(c + 1) * P], hk[:, c - 1, :],
                                  start=False, stop=False, skip_group_check=True)
                    for a in range(2):
                        mm = pe.matmul(T0[:, c * P + a * M:c * P + (a + 1) * M], aT[:, a, c, :],
                                       e_tok[:, c, a * M:(a + 1) * M], start=(c == 0 and a == 0),
                                       stop=(c == CH - 1 and a == 1), skip_group_check=True)
                mm.then_inc(s_ok, 1)
                pe.wait_ge(s_v, (u + 1) * CH)
                if tail and i >= 2:
                    pe.wait_ge(s_nl, CH * (i - 2) + (2 if last else CH))
                for c in range(CH - 1):
                    dst = (T1[:, 0:256], T1[:, 256:512], T3[:, 0:256])[c]
                    mm = pe.matmul(dst, e_tok[:, c, :], v[par][:, c, :], start=True, stop=True)
                mm.then_inc(s_hvd, 1)
                if not first:
                    out_transposes(u - 1)
                if not last:
                    job(QT, nu, ni)
                else:
                    norm_transposes(i - 2, (2, 3), (PJ[1], T2))
                if not first:
                    pe.wait_ge(s_ctok, u + 1)
                    if last:
                        pe.wait_ge(s_nl, CH * (i - 1))
                    out_product(u - 1, wo_ready(u, i))
                if first:
                    job(VG1, nu, ni)
                pe.wait_ge(s_okn, 6 * (u + 1))
                if not first:
                    pe.wait_ge(s_ya, u * CH - 3)
                for c in range(CH):
                    mm = pe.transpose(T2[:, c * P:(c + 1) * P], p[:, c * P:(c + 1) * P], ident[:, :])
                mm.then_inc(s_trw, 1)
                if not last:
                    if not first:
                        job(VG1, nu, ni)
                    job(KTJ, nu, ni)
                else:
                    early_product(0, 1)
                pe.wait_ge(s_wT, u + 1)
                if not first:
                    pe.wait_ge(s_ya, u * CH)
                for c in range(CH):
                    for a in range(2):
                        hs, cs = slice(M * a, M * (a + 1)), slice(c * P, (c + 1) * P)
                        mm = pe.matmul(A[a][:, cs], eT[par][hs, cs], wT[hs, cs], start=True, stop=True)
                mm.then_inc(s_b, 1)
                if not last:
                    job(VG2, nu, ni)
                pe.wait_ge(s_bm, 2 * (u + 1))
                pe.wait_ge(s_hv, 3 * (u + 1))
                for c in range(CH):
                    bk, at = (T1, T3)[c // 2], (c % 2) * 2 * DV
                    if c:
                        mm = pe.matmul(bk[:, at:at + 2 * DV], wT[:, c * P:(c + 1) * P], hv[:, c - 1, :],
                                       start=(c == 2), stop=False, skip_group_check=True)
                    for a in range(2):
                        mm = pe.matmul(bk[:, at + a * DV:at + (a + 1) * DV], aT[:, a, c, :],
                                       v[par][:, c, a * DV:(a + 1) * DV], start=(c == 0 and a == 0),
                                       stop=(a == 1 and c % 2 == 1), skip_group_check=True)
                    if c % 2:
                        mm.then_inc(s_o, 1)
                if not last:
                    job(VG3, nu, ni)

            def wo_ready(u, i):
                if i % B != 1:
                    return None
                return 5 * (u // B if isinstance(u, int) else pair_reg[0]) + 5

            def early_product(f, n):
                pe.wait_ge(s_early[n], 16)
                mm = gate_up_product(pe, bank[2 * f + n], (vgh, vgl)[n], f * P, xh, xl, 0)
                if n:
                    mm.then_inc(s_gu, 1)

            def norm_transposes(b, tiles, banks):
                for c, dst in zip(tiles, banks):
                    t = CH * b + c
                    pe.wait_ge(s_n, t + 1)
                    if c < 2 and b < 2:
                        pe.wait_ge((s_etok, s_ctok)[c], UNITS - 1 + b)
                    for k in range(KT):
                        mm = pe.transpose(dst[:, k * P:(k + 1) * P], norm_tile(t)[:, k * P:(k + 1) * P], ident[:, :])
                    mm.then_inc(s_ntr, 1)

            def token_transposes(t):
                pe.wait_ge(s_xn, t + 1)
                if t >= 4:
                    pe.wait_ge(s_xl, t - 3)
                for k in range(KT):
                    mm = pe.transpose(bank[4 + t % 4][:, k * P:(k + 1) * P], token_tile(t)[:, k * P:(k + 1) * P],
                                      ident[:, :])
                mm.then_inc(s_xtr, 1)

            pe.wait_ge(s_const, 4)
            for t in range(CH):
                token_transposes(t)
            for j in range(JOBS):
                job(j, 0, 0)
                for t in tokens_after(j):
                    token_transposes(t)
            pe.wait_ge(s_xl, TILES)
            unit(0, 0)
            with pe.Fori(0, PAIRS - 1) as h:
                pair_reg[0] = h
                for i in range(1, B + 1):
                    unit(h * B + i, i)
            for i in range(1, B):
                unit((PAIRS - 1) * B + i, i, last=(i == B - 1), tail=True)
            norm_transposes(2, (0, 1), (T0, T2))
            pe.wait_ge(s_sq, 2 * CH * UNITS)
            norm_transposes(2, (2, 3), (T1, T3))
            pe.wait_ge(s_bm, 2 * UNITS)
            for n in range(2):
                early_product(1, n)
            out_transposes(UNITS - 1, (T1, T3))
            out_product(UNITS - 1, None, (T1, T3))

        @block.scalar
        def _(act):
            def copy(dst, src):
                return act.activation(dst, src, ACT.Copy)

            def split_w(n, dst, count):
                act.wait_ge(s_stage, 16 * count)
                copy(dst, stage[:, :].rearrange("p (k n) -> p k n", k=KT)).then_inc(s_wh, 1)

            def split_next_w(n, j, nu):
                act.wait_ge(s_job, nu * JOBS + j + 1)
                split_w(n, wh["sqk"[n]][:, :, :], (h_of[0] + 1) * 5 + n + 1)

            def split_vg(pair, k):
                act.wait_ge(s_stage_vg[k], (pair + 1) * 32)
                copy(vgh[:, k, :], stage_vg[:, k, :]).then_inc(s_vgh, 1)

            def split_o(pair, a):
                act.wait_ge(s_stage, (pair * 5 + 4 + a) * 16)
                act.activation(stage[:, :], stage[:, :], ACT.Copy, scale=half_gn[:, 0:1]).then_inc(s_wos, 1)
                act.wait_ge(s_wos, pair * 2 + a + 1)
                copy(woh[:, a, :], stage[:, :]).then_inc(s_wh, 1)

            def evac(j, u, i):
                par = i % 2
                src = PJ[(JOBS * i + j) % 2]
                first = isinstance(u, int) and u == 0
                if j == ST:
                    act.wait_ge(s_clip, u + 1)
                    act.activation(eT[par][:, :], eT[par][:, :], ACT.Exp).then_inc(s_e, 1)
                    return
                act.wait_ge(s_job, u * JOBS + j + 1)
                if j == QT:
                    if not first:
                        act.wait_ge(s_ok, u)
                    copy(qT[:, :], src[:, :]).then_inc(s_q, 1)
                elif j == KTJ:
                    if not first:
                        act.wait_ge(s_a, u)
                    copy(kT[:, :], src[:, :]).then_inc(s_k, 1)
                else:
                    c = {VG0: 0, VG1: 1, VG2: 2, VG3: 3}[j]
                    if not isinstance(u, int) or u >= 2:
                        act.wait_ge(s_o, 2 * (u - 1))
                    copy(v[par][:, c, :], src[:, 0:2 * DV]).then_inc(s_v, 1)
                    if not (first and c == 0):
                        act.wait_ge(s_g, u * CH + c)
                    act.activation(th[:, :], src[:, 2 * DV:4 * DV], ACT.Tanh, scale=0.5).then_inc(s_th, 1)

            def norm_hi(b, tiles, banks):
                for c, src in zip(tiles, banks):
                    t = CH * b + c
                    act.wait_ge(s_ntr, t + 1)
                    copy(xh[:, :, t * P:(t + 1) * P], src[:, :].rearrange("p (k t) -> p k t", k=KT)
                         ).then_inc(s_nh, 1)

            def out_hi(u, banks=A):
                for a in range(2):
                    act.wait_ge(s_tro, 2 * u + a + 1)
                    copy(oh[:, a, :], banks[a][:, :]).then_inc(s_oh, 1)

            def unit(u, i, last=False, tail=False):
                first = isinstance(u, int) and u == 0
                nu, ni = u + 1, i + 1
                act.wait_ge(s_trk, u + 1)
                if not first:
                    act.wait_ge(s_hkd, u)
                copy(k_tok[:, :, :].rearrange("p c m -> p (c m)"), T0[:, :]).then_inc(s_ktok, 1)
                if i == 3 and not tail:
                    act.wait_ge(s_job, u * JOBS + VG3 + 1)
                    for k in range(KT):
                        split_vg(h_of[0] + 1, k)
                act.wait_ge(s_tre, u + 1)
                if not first:
                    act.wait_ge(s_hvd, u)
                copy(e_tok[:, :, :].rearrange("p c m -> p (c m)"), T1[:, :]).then_inc(s_etok, 1)
                act.wait_ge(s_trc, u + 1)
                if not first:
                    act.wait_ge(s_okn, 6 * (u - 1) + 1)
                copy(c_inv[:, :, :].rearrange("p c m -> p (c m)"), T2[:, :]).then_inc(s_ctok, 1)
                if not last:
                    evac(ST, nu, ni)
                if tail and i >= 2:
                    norm_hi(i - 2, (0, 1), (T1, T2))
                projections, outputs = split_next(i, tail)
                if not last:
                    evac(VG0, nu, ni)
                if tail and i >= 2 and not last:
                    norm_hi(i - 2, (2, 3), (T1, T2))
                if not first:
                    out_hi(u - 1)
                act.wait_ge(s_okn, 6 * u + 3)
                act.activation(p[:, :], p[:, :], ACT.Exp).then_inc(s_exp, 1)
                if last:
                    norm_hi(i - 2, (2, 3), (PJ[1], T2))
                if projections:
                    split_next_w(0, ST, nu)
                if not last:
                    evac(QT, nu, ni)
                    evac(VG1, nu, ni)
                if projections:
                    split_next_w(1, QT, nu)
                if outputs:
                    if not first:
                        act.wait_ge(s_y, CH * u)
                    split_o(0 if first else h_of[0] + 1, 0)
                if not last:
                    evac(KTJ, nu, ni)
                if projections:
                    split_next_w(2, KTJ, nu)
                if not last:
                    evac(VG2, nu, ni)
                if outputs:
                    split_o(0 if first else h_of[0] + 1, 1)
                if not first:
                    act.wait_ge(s_tro, 2 * u)
                    act.wait_ge(s_rstd, u)
                for k in range(2):
                    act.wait_ge(s_o, 2 * u + k + 1)
                    copy(o[:, 2 * k:2 * k + 2, :].rearrange("p a d -> p (a d)"), (T1, T3)[k][:, :]
                         ).then_inc(s_ocp, 1)
                    act.wait_ge(s_ocp, 2 * u + k + 1)
                    for c in (2 * k, 2 * k + 1):
                        for a in range(2):
                            at = (c % 2) * 2 * DV + a * DV
                            head = (T1, T3)[k][:, at:at + DV]
                            act.activation(head, head, ACT.Square,
                                           accum_out=ssq[:, 2 * c + a:2 * c + a + 1]).then_inc(s_sq, 1)
                if not last:
                    evac(VG3, nu, ni)

            h_of = [0]
            def token_hi(t):
                act.wait_ge(s_xtr, t + 1)
                copy(xh[:, :, t * P:(t + 1) * P],
                     bank[4 + t % 4][:, :].rearrange("p (k t) -> p k t", k=KT)).then_inc(s_xh, 1)

            split_w(0, wh["s"][:, :, :], 1)
            for t in range(CH):
                token_hi(t)
            for k in range(KT):
                split_vg(0, k)
            act.wait_ge(s_gn, 16)
            act.mul(half_gn[:, :], half_gn[:, :], 0.5).then_inc(s_gnh, 1)
            for j in range(JOBS):
                evac(j, 0, 0)
                if j == ST:
                    split_w(1, wh["q"][:, :, :], 2)
                for t in tokens_after(j):
                    token_hi(t)
                if j == VG0:
                    split_w(2, wh["k"][:, :, :], 3)
            act.wait_ge(s_gnh, 1)
            unit(0, 0)
            with act.Fori(0, PAIRS - 1) as h:
                h_of[0] = h
                for i in range(1, B + 1):
                    unit(h * B + i, i)
            for i in range(1, B):
                unit((PAIRS - 1) * B + i, i, last=(i == B - 1), tail=True)
            norm_hi(2, (0, 1), (T0, T2))
            norm_hi(2, (2, 3), (T1, T3))
            act.wait_ge(s_sc, 32)
            act.mul(gs[:, :], gs[:, :], 0.5).then_inc(s_hgs, 1)
            out_hi(UNITS - 1, (T1, T3))

        @block.gpsimd
        def _(pool):
            pool.memset(ident[:, :], 1.0).then_inc(s_const, 1)
            pool.wait_ge(s_const, 1)
            pool.affine_select(out=ident[:, :], in_=ident[:, :], compare_op=ALU.is_equal, fill=0.0, base=0,
                               pattern=[[1, P]], channel_multiplier=-1).then_inc(s_const, 1)
            pool.memset(tri[:, :], 1.0).then_inc(s_const, 1)
            pool.memset(neg_half[:, :], -0.5).then_inc(s_neg, 1)
            pool.wait_ge(s_neg, 1)
            pool.wait_ge(s_const, 3)
            pool.affine_select(out=tri[:, :], in_=tri[:, :], compare_op=ALU.is_ge, fill=0.0, base=0,
                               pattern=[[1, P]], channel_multiplier=-1).then_inc(s_const, 1)

            def lo(n, w_lo, w_hi, w):
                pool.wait_ge(s_wh, n)
                pool.tensor_tensor(w_lo, w, w_hi.bitcast(F32), ALU.subtract).then_inc(s_wl, 1)

            def lo_w(n, pair):
                name = "sqk"[n]
                lo(pair * 5 + n + 1, wl[name][:, :, :], wh[name][:, :, :],
                   stage[:, :].rearrange("p (k n) -> p k n", k=KT))

            def lo_vg(pair, k):
                pool.wait_ge(s_vgh, pair * KT + k + 1)
                pool.tensor_tensor(vgl[:, k, :], stage_vg[:, k, :], vgh[:, k, :].bitcast(F32), ALU.subtract
                                   ).then_inc(s_vgl2, 1)

            def unit(u, i, last=False, tail=False):
                projections, outputs = split_next(i, tail)
                first = isinstance(u, int) and u == 0
                if not first:
                    rsqrt(u - 1)
                if i == 3 and not tail:
                    pool.wait_ge(s_job, u * JOBS + VG3 + 1)
                    for k in range(2, KT):
                        lo_vg(h_of[0] + 1, k)
                if projections:
                    for n in range(3):
                        lo_w(n, h_of[0] + 1)
                if outputs:
                    pair = 0 if first else h_of[0] + 1
                    for a in range(2):
                        if not first:
                            pool.wait_ge(s_y, CH * u)
                        lo(pair * 5 + 4 + a, wol[:, a, :], woh[:, a, :], stage[:, :])

            def norm_rsqrt(b, n, cols=slice(0, CH)):
                pool.wait_ge(s_var, n + 1)
                pool.tensor_tensor(sd[b][:, cols], sd[b][:, cols], neg_half[:, cols], ALU.pow).then_inc(s_sd, 1)

            def rsqrt(u):
                pool.wait_ge(s_ms, u + 1)
                pool.tensor_tensor(rstd[:, :], ssq[:, :], neg_half[:, :], ALU.pow).then_inc(s_rstd, 1)

            h_of = [0]
            norm_rsqrt(0, 0, slice(0, 2))
            norm_rsqrt(0, 1, slice(2, CH))
            lo_w(0, 0)
            for k in range(2, KT):
                lo_vg(0, k)
            norm_rsqrt(1, 2)
            lo_w(1, 0)
            norm_rsqrt(2, 3)
            lo_w(2, 0)
            norm_rsqrt(3, 4)
            unit(0, 0)
            with pool.Fori(0, PAIRS - 1) as h:
                h_of[0] = h
                for i in range(1, B + 1):
                    unit(h * B + i, i)
            for i in range(1, B):
                unit((PAIRS - 1) * B + i, i, last=(i == B - 1), tail=True)
                norm_rsqrt(i - 1, B + i)
            rsqrt(UNITS - 1)
            pool.wait_ge(s_last_var, 1)
            pool.tensor_tensor(last_sd, last_sd, neg_half[:, 0:CH], ALU.pow)

        @block.vector
        def _(dve):
            tri4 = tri[:, :].rearrange("p (c t) -> p c t", c=1).broadcast_to([P, CH, P])

            def lo(dst, src, hi):
                return dve.tensor_tensor(dst, src, hi.bitcast(F32), ALU.subtract)

            def lo_vg(pair, k):
                dve.wait_ge(s_vgh, pair * KT + k + 1)
                lo(vgl[:, k, :], stage_vg[:, k, :], vgh[:, k, :]).then_inc(s_vgl, 1)

            def clip(u, i):
                dve.wait_ge(s_job, u * JOBS + ST + 1)
                if not isinstance(u, int) or u >= 2:
                    dve.wait_ge(s_b, u - 1)
                dve.tensor_scalar(eT[i % 2][:, :], PJ[(JOBS * i + ST) % 2][:, :], -CLAMP, CLAMP,
                                  ALU.max, ALU.min).then_inc(s_clip, 1)

            def sums(u, i):
                dve.wait_ge(s_e, u + 1)
                if not isinstance(u, int) or u >= 2:
                    dve.wait_ge(s_trc, u - 1)
                dve.tensor_tensor_scan(cT[i % 2][:, :], eT[i % 2][:, :], eT[i % 2][:, :], 0.0, ALU.add,
                                       ALU.bypass).then_inc(s_scan, 1)
                dve.wait_ge(s_scan, u + 1)
                dve.reciprocal(cT[i % 2][:, :], cT[i % 2][:, :]).then_inc(s_cinv, 1)

            def gate(c, u, i):
                if not isinstance(u, int) or u >= 2:
                    dve.wait_ge(s_og, u - 1)
                dve.wait_ge(s_th, u * CH + c + 1)
                dve.scalar_tensor_tensor(out=g[i % 2][:, c, :], in0=th[:, :], scalar=1.0,
                                         in1=PJ[(JOBS * i + (VG0, VG1, VG2, VG3)[c]) % 2][:, 2 * DV:4 * DV],
                                         op0=ALU.add, op1=ALU.mult).then_inc(s_g, 1)

            def mask(u, s_in, s_out, used, count):
                dve.wait_ge(s_in, u + 1)
                if count is not None:
                    dve.wait_ge(used, count)
                for a in range(2):
                    dve.tensor_tensor(aT[:, a, :, :], A[a][:, :].rearrange("p (c t) -> p c t", c=CH), tri4,
                                      ALU.mult).then_inc(s_out, 1)

            def states(u, dst, width, parts, s_step):
                for c in range(CH - 1):
                    if c:
                        dve.wait_ge(s_step, u * 3 + c)
                    for a in range(2):
                        rows, cols = slice(64 * a, 64 * (a + 1)), slice(width * a, width * (a + 1))
                        src = parts(c)[rows, cols]
                        if c == 0:
                            st = dve.tensor_copy(dst[rows, c, cols], src)
                        else:
                            st = dve.tensor_tensor(dst[rows, c, cols], src, dst[rows, c - 1, cols], ALU.add)
                    st.then_inc(s_step, 1)

            def mean_square(u):
                dve.wait_ge(s_sq, 8 * (u + 1))
                dve.tensor_scalar(ssq[:, :], ssq[:, :], 1.0 / DV, EPS, ALU.mult, ALU.add).then_inc(s_ms, 1)

            def norm_gate(u, i):
                dve.wait_ge(s_rstd, u + 1)
                for c in range(CH):
                    for a in range(2):
                        blk = o[:, c, a * DV:(a + 1) * DV]
                        st = dve.scalar_tensor_tensor(out=blk, in0=blk, scalar=rstd[:, 2 * c + a:2 * c + a + 1],
                                                      in1=g[i % 2][:, c, a * DV:(a + 1) * DV],
                                                      op0=ALU.mult, op1=ALU.mult)
                st.then_inc(s_og, 1)

            def out_lo(u, banks=A):
                for a in range(2):
                    dve.wait_ge(s_oh, 2 * u + a + 1)
                    lo(ol[:, a, :], banks[a][:, :], oh[:, a, :]).then_inc(s_ol, 1)

            def add_y(u, i, c, banks=A):
                dve.wait_ge(s_y, CH * u + c + 1)
                t = CH * (i % B) + c
                dve.tensor_tensor(y[:, t, :], y[:, t, :], (T2, banks[0], banks[1], T0)[c][:, :], ALU.add
                                  ).then_inc(s_ya, 1)

            def norm_statistics(b):
                dve.wait_ge(s_ya, CH * (UNITS - B + b + 1))
                if b == 0:
                    dve.wait_ge(s_fp8_out, 16 * (UNITS - B + 1))
                norm_stats(dve, y, b, stats[b], mv[b], sd[b], (s_mv, 2 * (B + b + 1)), s_var)

            def norm_tokens(b, tiles):
                dve.wait_ge(s_sd, B + b + 2)
                for c in tiles:
                    t = CH * b + c
                    if t >= 2 and t - 2 * CH not in (2, 3):
                        dve.wait_ge(s_ntr, t - 1)
                    dve.tensor_scalar(norm_tile(t), y[:, t, :], mv[b][:, c, 0:1], sd[b][:, c:c + 1],
                                      ALU.subtract, ALU.mult).then_inc(s_n, 1)

            def norm_lo(b, tiles, banks):
                for c, src in zip(tiles, banks):
                    t = CH * b + c
                    dve.wait_ge(s_nh, t + 1)
                    cols = slice(t * P, (t + 1) * P)
                    lo(xl[:, :, cols], src[:, :].rearrange("p (k t) -> p k t", k=KT), xh[:, :, cols]
                       ).then_inc(s_nl, 1)

            def quantise(u, steps):
                n_q = QC0 if isinstance(u, int) else QC
                w, t = (q[:, :, 0:n_q] for q in (q8, q8t))
                todo = (
                    lambda: dve.tensor_scalar(t.bitcast(I32), w.bitcast(I32), 0x7F800000, None, ALU.bitwise_and),
                    lambda: dve.tensor_scalar(t, t, FP8_MIN_NORMAL, ROUNDER, ALU.max, ALU.mult),
                    lambda: dve.tensor_tensor(w, w, t, ALU.add),
                    lambda: dve.tensor_tensor(w, w, t, ALU.subtract),
                    lambda: dve.tensor_tensor(t, w, w, ALU.mult),
                    lambda: dve.tensor_scalar(t, t, FP8_MAX ** 2, FP8_MAX ** 2, ALU.max, ALU.subtract),
                    lambda: dve.tensor_scalar(t, t, HUGE, HUGE, ALU.mult, ALU.mult),
                    lambda: dve.scalar_tensor_tensor(out=w, in0=t, scalar=0.0, in1=w, op0=ALU.mult, op1=ALU.add))
                for n in range(Q8_STEPS)[steps]:
                    if n == 0:
                        dve.wait_ge(s_q8in, (u + 1) * 48)
                    else:
                        dve.wait_ge(s_q8, u * Q8_STEPS + n)
                    todo[n]().then_inc(s_q8, 1)

            def unit(u, i, last=False, tail=False):
                first = isinstance(u, int) and u == 0
                nu, ni = u + 1, i + 1
                if i == 3 and not tail:
                    dve.wait_ge(s_job, u * JOBS + VG3 + 1)
                    for k in range(2):
                        lo_vg(h_of[0] + 1, k)
                mask(u, s_a, s_am, s_o, None if first else 2 * u)
                if not first and not last:
                    norm_gate(u - 1, i - 1)
                if not last:
                    clip(nu, ni)
                dve.wait_ge(s_hkd, u + 1)
                if not first:
                    dve.wait_ge(s_ok, u)
                states(u, hk, DK, lambda c: T3[:, c * P:(c + 1) * P], s_hk)
                if last:
                    norm_gate(u - 1, i - 1)
                if tail and i >= 2:
                    norm_lo(i - 2, (0, 1), (T1, T2))
                    norm_tokens(i - 2, (2, 3))
                if not tail:
                    sums(nu, ni)
                if not last:
                    gate(0, nu, ni)
                if tail and i >= 2 and not last:
                    norm_lo(i - 2, (2, 3), (T1, T2))
                k = [6 * u]

                def step(ins, wait=True):
                    k[0] += 1
                    ins.then_inc(s_okn, 1)
                    if wait:
                        dve.wait_ge(s_okn, k[0])

                p3 = p[:, :].rearrange("p (s m) -> p s m", m=M)
                dve.wait_ge(s_ok, u + 1)
                dve.wait_ge(s_ctok, u + 1)
                if not first:
                    dve.wait_ge(s_trw, u)
                step(dve.scalar_tensor_tensor(out=p[:, :], in0=T0[:, :], scalar=SCALE,
                                              in1=c_inv[:, :, :].rearrange("p c m -> p (c m)"),
                                              op0=ALU.mult, op1=ALU.mult))
                step(dve.tensor_reduce(mx[:, :], p3, AX.X, ALU.max))
                step(dve.tensor_tensor(p3, p3, mx[:, :].rearrange("p (s a) -> p s a", a=1).broadcast_to(
                    [P, 2 * CH, M]), ALU.subtract), wait=False)
                if not first:
                    out_lo(u - 1)
                if last:
                    norm_lo(i - 2, (2, 3), (PJ[1], T2))
                dve.wait_ge(s_hvd, u + 1)
                if not first:
                    dve.wait_ge(s_o, 2 * u)
                states(u, hv, DV, lambda c: (T1[:, 0:256], T1[:, 256:512], T3[:, 0:256])[c], s_hv)
                dve.wait_ge(s_exp, u + 1)
                step(dve.tensor_reduce(sm[:, :], p3, AX.X, ALU.add))
                step(dve.reciprocal(rs[:, :], sm[:, :]))
                step(dve.tensor_tensor(p3, p3, rs[:, :].rearrange("p (s a) -> p s a", a=1).broadcast_to(
                    [P, 2 * CH, M]), ALU.mult), wait=False)
                if not first:
                    for c in range(CH):
                        add_y(u - 1, i - 1, c)
                dve.wait_ge(s_trw, u + 1)
                if not first:
                    dve.wait_ge(s_o, 2 * u)
                dve.tensor_tensor(wT[:, :], T2[:, :], cT[i % 2][:, :], ALU.mult).then_inc(s_wT, 1)
                if not last:
                    gate(1, nu, ni)
                    if tail:
                        sums(nu, ni)
                if not tail:
                    quantise(u, slice(0, 5))
                mask(u, s_b, s_bm, s_ok, u + 1)
                if not tail:
                    quantise(u, slice(5, Q8_STEPS))
                if tail:
                    norm_statistics(i - 1)
                if not last:
                    gate(2, nu, ni)
                if tail:
                    norm_tokens(i - 1, range(CH) if last else (0, 1))
                mean_square(u)
                if not last:
                    gate(3, nu, ni)

            def batch_3_stats(c):
                dve.wait_ge(s_ya, CH * (UNITS - 1) + c + 1)
                st = dve.bn_stats(stats[B - 1][:, c, :], y[:, CH * (B - 1) + c, :])
                if c == CH - 1:
                    st.then_inc(s_mv, 1)

            h_of = [0]
            dve.memset(hk[:, :, :], 0.0)
            dve.memset(hv[:, :, :], 0.0).then_inc(s_zero, 1)
            dve.wait_ge(s_zero, 1)

            def x_lo(t):
                dve.wait_ge(s_xh, t + 1)
                lo(xl[:, :, t * P:(t + 1) * P], bank[4 + t % 4][:, :].rearrange("p (k t) -> p k t", k=KT),
                   xh[:, :, t * P:(t + 1) * P]).then_inc(s_xl, 1)

            def token_stats(b):
                norm_stats(dve, y, b, stats[b], mv[b], sd[b], (s_mv, 2 * (b + 1)), s_var, CH * [(s_x[b], 16)])

            def token_norm(t):
                b, c = t // CH, t % CH
                dve.wait_ge(s_sd, b + 2 if t >= 2 else 1)
                if t >= 4:
                    dve.wait_ge(s_xtr, t - 3)
                dve.tensor_scalar(token_tile(t), y[:, t, :], mv[b][:, c, 0:1], sd[b][:, c:c + 1],
                                  ALU.subtract, ALU.mult).then_inc(s_xn, 1)

            for n in range(2):
                norm_stats(dve, y, 0, stats[0], mv[0], sd[0], (s_mv, 2 * n), s_var, [(s, 16) for s in s_x0],
                           range(2 * n, 2 * n + 2))
            for t in range(CH):
                token_norm(t)
            for t in range(CH):
                x_lo(t)
            for k in range(2):
                lo_vg(0, k)
            token_stats(1)
            clip(0, 0)
            for t in range(CH, 2 * CH):
                token_norm(t)
            for b in range(1, B):
                if b + 1 < B:
                    token_stats(b + 1)
                gate(b - 1, 0, 0)
                for t in range(CH * b, CH * (b + 1)):
                    x_lo(t)
                    if t % 2 and b + 1 < B:
                        token_norm(t + 3)
                        token_norm(t + 4)
            sums(0, 0)
            gate(B - 1, 0, 0)
            dve.wait_ge(s_const, 4)
            unit(0, 0)
            with dve.Fori(0, PAIRS - 1) as h:
                h_of[0] = h
                for i in range(1, B + 1):
                    unit(h * B + i, i)
            for i in range(1, B):
                unit((PAIRS - 1) * B + i, i, last=(i == B - 1), tail=True)
            norm_lo(2, (0, 1), (T0, T2))
            norm_lo(2, (2, 3), (T1, T3))
            norm_gate(UNITS - 1, B - 1)
            out_lo(UNITS - 1, (T1, T3))
            for c in range(CH):
                add_y(UNITS - 1, B - 1, c, (T1, T3))
                if c:
                    batch_3_stats(c - 1)
            batch_3_stats(CH - 1)
            dve.wait_ge(s_sc, 32)
            dve.wait_ge(s_hgs, 1)
            dve.tensor_tensor(us[:, :], us[:, :], gs[:, :], ALU.mult)
            norm_aggregate(dve, stats[B - 1], last_mv, last_sd, (s_mv, 4 * B), s_last_var)


def feed_forward(nc, sb_top, sem, fp8_scratch, down_s, out, shared):
    y, ident, bank, xh, xl, wg0, wu0, neg_half, _, _, mv, sd, hgs, gus, s_early, s_gu = shared
    Y = bank[4:8]
    NB = B - 1
    with ExitStack() as ctx:
        def sb(name, shape, dt=F32):
            return sb_top(name, shape, dt, ctx)

        wg, wu = (sb(n, [P, KT, F - EARLY * P], F32R) for n in ("w_gate", "w_up"))
        wd = sb("w_down", [P, FT, D], F32R)
        xn = sb("xn", [P, CH, D])
        ds_row = sb("down_scale", [P, D])
        th, ga = (sb(n, [P, 2, T]) for n in ("tanh_half", "gated"))
        fh, fl = (sb(n, [P, 2, T], F32R) for n in ("fuse_hi", "fuse_lo"))
        res = sb("result", [P, CH, D])

        PARTS = FT // EARLY
        s_wgu = [sem(f"gate_up_loaded{n}") for n in range(PARTS)]
        s_wd = [sem(f"down_loaded{n}") for n in range(PARTS)]
        s_ds = sem("down_scale_loaded")
        s_xn, s_xtr, s_xh, s_xl = sem("n3_ready"), sem("n3_transposed"), sem("n3T_hi_ready"), sem("n3T_lo_ready")
        s_th, s_ga, s_fu = sem("tanh2_ready"), sem("gated_ready"), sem("fuse_ready")
        s_fh, s_fl, s_dn = sem("fuse_hi_ready"), sem("fuse_lo_ready"), sem("down_done")
        s_bank = sem("output_bank_done")
        s_ys, s_res, s_out = sem("y_scaled"), sem("result_ready"), sem("result_stored")

        block = ctx.enter_context(nc.Block())

        def blocks(eng, tokens):
            tokens(0, first=True)
            with eng.Fori(1, B - 1) as b:
                tokens(b)
            tokens(B - 1, last=True)

        @block.sync
        def _(sp):
            down = fp8_scratch[2].rearrange("p c -> (p c)").rearrange("(k q n) -> q k n", k=FT, q=P)
            for n in range(PARTS):
                f0, f1 = n * EARLY, (n + 1) * EARLY
                if n:
                    for m, w in enumerate((wg, wu)):
                        sp.dma_start(w[:, :, (f0 - EARLY) * P:(f1 - EARLY) * P].bitcast(F32),
                                     gate_up_columns(fp8_scratch[m], KT, f0, f1)).then_inc(s_wgu[n], 16)
                sp.dma_start(wd[:, f0:f1, :].bitcast(F32), down[:, f0:f1, :]).then_inc(s_wd[n], 16)
                if n == 0:
                    sp.dma_start(ds_row[:, :], down_s.rearrange("(a n) -> a n", a=1).broadcast_to([P, D])
                                 ).then_inc(s_ds, 16)
            with sp.Fori(0, B) as b:
                for c in range(CH):
                    sp.wait_ge(s_res, b * CH + c + 1)
                    sp.dma_start(out.rearrange("b (c p) d -> (b c) p d", p=P)[bass.ds(b * CH + c, 1), :, :]
                                 .rearrange("a p d -> (a p) d"), res[:, c, :]).then_inc(s_out, 16)
            sp.wait_ge(s_out, 16 * TILES)

        @block.tensor
        def _(pe):
            def gate_up(b, f, first):
                pe.wait_ge(s_fu, b * FT + f - 1)
                if first and f % EARLY == 0:
                    pe.wait_ge(s_wgu[f // EARLY], 32)
                at = (f if f < EARLY else f - EARLY) * P
                for n, w in enumerate((wg0, wu0) if f < EARLY else (wg, wu)):
                    mm = gate_up_product(pe, bank[2 * (f % 2) + n], w, at, xh, xl, b)
                mm.then_inc(s_gu, 1)

            def tokens(b, first=False, last=False):
                for f in range(FT):
                    if first and f == 0:
                        for c in range(CH):
                            pe.wait_ge(s_xn, c + 1)
                            for k in range(KT):
                                mm = pe.transpose(Y[c][:, k * P:(k + 1) * P], xn[:, c, k * P:(k + 1) * P],
                                                  ident[:, :])
                            mm.then_inc(s_xtr, 1)
                    if f + 2 < FT:
                        gate_up(b, f + 2, first)
                    elif not last:
                        gate_up(b + 1, f + 2 - FT, False)
                    if first and f == 0:
                        pe.wait_ge(s_xl, CH)
                    pe.wait_ge(s_fh, b * FT + f + 1)
                    pe.wait_ge(s_fl, b * FT + f + 1)
                    if first and f % EARLY == 0:
                        pe.wait_ge(s_wd[f // EARLY], 16)
                    for c in range(CH):
                        if f == 0 and not first:
                            pe.wait_ge(s_ys, (b - 1) * CH + c + 1)
                        for part in (fh, fl):
                            mm = pe.matmul(Y[c][:, :], part[:, f % 2, c * P:(c + 1) * P], wd[:, f, :],
                                           start=(f == 0 and part is fh), stop=(f == FT - 1 and part is fl))
                        if c + 1 < CH and f == FT - 1:
                            mm.then_inc(s_bank, 1)
                    mm.then_inc(s_dn, 1)

            blocks(pe, tokens)

        @block.scalar
        def _(act):
            def feature(b, f, early):
                act.wait_ge(s_gu, b * FT + f + 1)
                if not early:
                    act.wait_ge(s_ga, b * FT + f - 1)
                act.activation(th[:, f % 2, :], bank[2 * (f % 2)][:, :], ACT.Tanh, scale=hgs[:, f:f + 1]
                               ).then_inc(s_th, 1)
                act.wait_ge(s_fu, b * FT + f + 1)
                if not early:
                    act.wait_ge(s_dn, b * FT + f - 1)
                act.activation(fh[:, f % 2, :], ga[:, f % 2, :], ACT.Copy).then_inc(s_fh, 1)

            def tokens(b, first=False, last=False):
                for f in range(FT):
                    feature(b, f, first and f < 2)
                    if first and f == 0:
                        for c in range(CH):
                            act.wait_ge(s_xtr, c + 1)
                            t = NB * CH + c
                            act.activation(xh[:, :, t * P:(t + 1) * P],
                                           Y[c][:, :].rearrange("p (k t) -> p k t", k=KT), ACT.Copy
                                           ).then_inc(s_xh, 1)

            blocks(act, tokens)

        @block.vector
        def _(dve):
            for c in range(CH):
                dve.tensor_scalar(xn[:, c, :], y[:, NB * CH + c, :], mv[:, c, 0:1], sd[:, c:c + 1],
                                  ALU.subtract, ALU.mult).then_inc(s_xn, 1)

            def fuse(b, f, early):
                dve.wait_ge(s_th, b * FT + f + 1)
                if not early:
                    dve.wait_ge(s_fl, b * FT + f - 1)
                    dve.wait_ge(s_fh, b * FT + f - 1)
                dve.scalar_tensor_tensor(out=ga[:, f % 2, :], in0=th[:, f % 2, :], scalar=1.0,
                                         in1=bank[2 * (f % 2)][:, :], op0=ALU.add, op1=ALU.mult
                                         ).then_inc(s_ga, 1)
                dve.wait_ge(s_ga, b * FT + f + 1)
                dve.scalar_tensor_tensor(out=ga[:, f % 2, :], in0=ga[:, f % 2, :], scalar=gus[:, f:f + 1],
                                         in1=bank[2 * (f % 2) + 1][:, :], op0=ALU.mult, op1=ALU.mult
                                         ).then_inc(s_fu, 1)
                dve.wait_ge(s_fh, b * FT + f + 1)
                dve.tensor_tensor(fl[:, f % 2, :], ga[:, f % 2, :], fh[:, f % 2, :].bitcast(F32),
                                  ALU.subtract).then_inc(s_fl, 1)

            def scale(b, first, tiles=range(CH)):
                for c in tiles:
                    if c + 1 < CH:
                        dve.wait_ge(s_bank, b * (CH - 1) + c + 1)
                    else:
                        dve.wait_ge(s_dn, b * FT + FT)
                    if first:
                        dve.wait_ge(s_ds, 16)
                    if not first:
                        dve.wait_ge(s_out, b * 16 * CH)
                    dve.tensor_tensor(res[:, c, :], Y[c][:, :], ds_row[:, :], ALU.mult).then_inc(s_ys, 1)

            def residual(b, first, tiles=range(CH)):
                for c in tiles:
                    dve.wait_ge(s_ys, b * CH + c + 1)
                    dve.tensor_tensor(res[:, c, :], res[:, c, :],
                                      y[:, c, :] if first else y[:, bass.ds(b * CH + c, 1), :].rearrange(
                                          "p a d -> p (a d)"), ALU.add).then_inc(s_res, 1)

            def tokens(b, first=False, last=False):
                for f in range(2, FT):
                    fuse(b, f, False)
                if last:
                    for c in range(CH):
                        scale(b, first, (c,))
                        residual(b, first, (c,))
                    return
                fuse(b + 1, 0, False)
                scale(b, first)
                fuse(b + 1, 1, False)
                residual(b, first)

            fuse(0, 0, True)
            for c in range(CH):
                dve.wait_ge(s_xh, c + 1)
                cols = slice((NB * CH + c) * P, (NB * CH + c + 1) * P)
                dve.tensor_tensor(xl[:, :, cols], Y[c][:, :].rearrange("p (k t) -> p k t", k=KT),
                                  xh[:, :, cols].bitcast(F32), ALU.subtract).then_inc(s_xl, 1)
            fuse(0, 1, True)
            blocks(dve, tokens)


_INS = ["L0_attn_hidden_states", "L0_attn_Wq", "L0_attn_Wk", "L0_attn_Wv", "L0_attn_Wg", "L0_attn_Ws",
        "L0_attn_Wo", "L0_attn_g_norm_weight", "L0_ffn_gate_w", "L0_ffn_up_w", "L0_ffn_down_w",
        "L0_ffn_gate_scale", "L0_ffn_up_scale", "L0_ffn_down_scale"]


def kernel(**inputs):
    import numpy as _np
    import concourse.bacc as _bacc
    from concourse import mybir as _mybir
    from concourse.bass_utils import run_bass_kernel_spmd as _run

    nc = _bacc.Bacc("TRN2", target_bir_lowering=False, num_devices=1)
    arrays, args = {}, []
    for name in _INS:
        a = _np.ascontiguousarray(inputs[name])
        arrays[f"in_{name}"] = a
        args.append(nc.dram_tensor(f"in_{name}", a.shape, _mybir.dt.from_np(a.dtype), kind="ExternalInput").ap())
    args.append(nc.dram_tensor("out_0", (B, T, D), F32, kind="ExternalOutput").ap())
    gsa_swiglu(nc, *args)
    r = _run(nc, [arrays], core_ids=[0])
    return r.results[0]["out_0"]
```
